# Optimizing a Trainium2 kernel written in Bass

```python
import numpy as np
import jax
import jax.numpy as jnp

def _softmax(x, axis=-1):
    return jax.nn.softmax(x, axis=axis)

def _gelu(x):
    return jax.nn.gelu(x, approximate=True)

def _silu(x):
    return jax.nn.silu(x)

def _sigmoid(x):
    return jax.nn.sigmoid(x)

def _layernorm(x, axis=-1, eps=1e-05):
    m = jnp.mean(x, axis=axis, keepdims=True)
    v = jnp.var(x, axis=axis, keepdims=True)
    return (x - m) / jnp.sqrt(v + eps)

def _scatter_add(tgt, idx, src, axis=0):
    return tgt.at[idx].add(src)

def _segment_sum(src, seg, n):
    return jax.ops.segment_sum(src, seg, n)
kernel_name = 'mk_dlrm_tower_d1_rec_r8_4e8bcf'

def setup_inputs(seed: int=0):
    np.random.seed(seed)
    _w = jnp.asarray

    def _rec_inputs():
        import jax
        import jax.numpy as jnp
        _tk = jax.random.key(seed)
        ids = jnp.stack([jax.random.randint(jax.random.fold_in(_tk, 200 + f), (512,), 0, v, jnp.int32) for f, v in enumerate([1250, 12500, 1000, 12500, 1000, 12500, 1000, 12500, 125000, 12500, 1250, 1000, 1000, 12500, 1250, 12500, 1000, 1250, 12500, 1250, 1000, 1000, 1000, 1000, 1250, 1250, 1250, 1250, 1000, 1250, 1000, 1250, 1000])], axis=1)
        tbl_0 = 0.05 * jax.random.normal(jax.random.fold_in(_tk, 500 + 0), (1250, 128), jnp.float32)
        tbl_1 = 0.05 * jax.random.normal(jax.random.fold_in(_tk, 500 + 1), (12500, 128), jnp.float32)
        tbl_2 = 0.05 * jax.random.normal(jax.random.fold_in(_tk, 500 + 2), (1000, 128), jnp.float32)
        tbl_3 = 0.05 * jax.random.normal(jax.random.fold_in(_tk, 500 + 3), (12500, 128), jnp.float32)
        tbl_4 = 0.05 * jax.random.normal(jax.random.fold_in(_tk, 500 + 4), (1000, 128), jnp.float32)
        tbl_5 = 0.05 * jax.random.normal(jax.random.fold_in(_tk, 500 + 5), (12500, 128), jnp.float32)
        tbl_6 = 0.05 * jax.random.normal(jax.random.fold_in(_tk, 500 + 6), (1000, 128), jnp.float32)
        tbl_7 = 0.05 * jax.random.normal(jax.random.fold_in(_tk, 500 + 7), (12500, 128), jnp.float32)
        tbl_8 = 0.05 * jax.random.normal(jax.random.fold_in(_tk, 500 + 8), (125000, 128), jnp.float32)
        tbl_9 = 0.05 * jax.random.normal(jax.random.fold_in(_tk, 500 + 9), (12500, 128), jnp.float32)
        tbl_10 = 0.05 * jax.random.normal(jax.random.fold_in(_tk, 500 + 10), (1250, 128), jnp.float32)
        tbl_11 = 0.05 * jax.random.normal(jax.random.fold_in(_tk, 500 + 11), (1000, 128), jnp.float32)
        tbl_12 = 0.05 * jax.random.normal(jax.random.fold_in(_tk, 500 + 12), (1000, 128), jnp.float32)
        tbl_13 = 0.05 * jax.random.normal(jax.random.fold_in(_tk, 500 + 13), (12500, 128), jnp.float32)
        tbl_14 = 0.05 * jax.random.normal(jax.random.fold_in(_tk, 500 + 14), (1250, 128), jnp.float32)
        tbl_15 = 0.05 * jax.random.normal(jax.random.fold_in(_tk, 500 + 15), (12500, 128), jnp.float32)
        tbl_16 = 0.05 * jax.random.normal(jax.random.fold_in(_tk, 500 + 16), (1000, 128), jnp.float32)
        tbl_17 = 0.05 * jax.random.normal(jax.random.fold_in(_tk, 500 + 17), (1250, 128), jnp.float32)
        tbl_18 = 0.05 * jax.random.normal(jax.random.fold_in(_tk, 500 + 18), (12500, 128), jnp.float32)
        tbl_19 = 0.05 * jax.random.normal(jax.random.fold_in(_tk, 500 + 19), (1250, 128), jnp.float32)
        tbl_20 = 0.05 * jax.random.normal(jax.random.fold_in(_tk, 500 + 20), (1000, 128), jnp.float32)
        tbl_21 = 0.05 * jax.random.normal(jax.random.fold_in(_tk, 500 + 21), (1000, 128), jnp.float32)
        tbl_22 = 0.05 * jax.random.normal(jax.random.fold_in(_tk, 500 + 22), (1000, 128), jnp.float32)
        tbl_23 = 0.05 * jax.random.normal(jax.random.fold_in(_tk, 500 + 23), (1000, 128), jnp.float32)
        tbl_24 = 0.05 * jax.random.normal(jax.random.fold_in(_tk, 500 + 24), (1250, 128), jnp.float32)
        tbl_25 = 0.05 * jax.random.normal(jax.random.fold_in(_tk, 500 + 25), (1250, 128), jnp.float32)
        tbl_26 = 0.05 * jax.random.normal(jax.random.fold_in(_tk, 500 + 26), (1250, 128), jnp.float32)
        tbl_27 = 0.05 * jax.random.normal(jax.random.fold_in(_tk, 500 + 27), (1250, 128), jnp.float32)
        tbl_28 = 0.05 * jax.random.normal(jax.random.fold_in(_tk, 500 + 28), (1000, 128), jnp.float32)
        tbl_29 = 0.05 * jax.random.normal(jax.random.fold_in(_tk, 500 + 29), (1250, 128), jnp.float32)
        tbl_30 = 0.05 * jax.random.normal(jax.random.fold_in(_tk, 500 + 30), (1000, 128), jnp.float32)
        tbl_31 = 0.05 * jax.random.normal(jax.random.fold_in(_tk, 500 + 31), (1250, 128), jnp.float32)
        tbl_32 = 0.05 * jax.random.normal(jax.random.fold_in(_tk, 500 + 32), (1000, 128), jnp.float32)
        _rk = jax.random.fold_in(_tk, 7)
        r_gnn_feature = -0.00340659 + 1.00146 * jax.random.normal(jax.random.fold_in(_rk, 101), (512, 128), jnp.float32)
        W_top1 = 0.051031 * jax.random.normal(jax.random.fold_in(_tk, 801), (384, 512), jnp.float32)
        W_top2 = 0.0441942 * jax.random.normal(jax.random.fold_in(_tk, 802), (512, 256), jnp.float32)
        W_top3 = 0.0625 * jax.random.normal(jax.random.fold_in(_tk, 803), (256, 1), jnp.float32)
        b_top1 = jnp.zeros((512,), jnp.float32)
        b_top2 = jnp.zeros((256,), jnp.float32)
        return (r_gnn_feature, ids, tbl_0, tbl_1, tbl_2, tbl_3, tbl_4, tbl_5, tbl_6, tbl_7, tbl_8, tbl_9, tbl_10, tbl_11, tbl_12, tbl_13, tbl_14, tbl_15, tbl_16, tbl_17, tbl_18, tbl_19, tbl_20, tbl_21, tbl_22, tbl_23, tbl_24, tbl_25, tbl_26, tbl_27, tbl_28, tbl_29, tbl_30, tbl_31, tbl_32, W_top1, b_top1, W_top2, b_top2, W_top3)
    r_gnn_feature, ids, tbl_0, tbl_1, tbl_2, tbl_3, tbl_4, tbl_5, tbl_6, tbl_7, tbl_8, tbl_9, tbl_10, tbl_11, tbl_12, tbl_13, tbl_14, tbl_15, tbl_16, tbl_17, tbl_18, tbl_19, tbl_20, tbl_21, tbl_22, tbl_23, tbl_24, tbl_25, tbl_26, tbl_27, tbl_28, tbl_29, tbl_30, tbl_31, tbl_32, W_top1, b_top1, W_top2, b_top2, W_top3 = _rec_inputs()

    def _L0_rec_setup():
        import jax, jax.numpy as jnp
        import numpy as np
        B, F, D, A = (1024, 33, 128, 128)
        key = jax.random.key(seed)
        k1, k2, k3, k4 = jax.random.split(key, 4)
        gnn_feature = jax.random.normal(k1, (B, A), dtype=jnp.float32)
        x = jax.random.normal(k2, (B, F, D), dtype=jnp.float32)
        lim = 1.0 / np.sqrt(D)
        attn_W = jax.random.uniform(k3, (A, D), minval=-lim, maxval=lim, dtype=jnp.float32)
        attn_b = jax.random.uniform(k4, (A,), minval=-lim, maxval=lim, dtype=jnp.float32)
        return {'gnn_feature': gnn_feature, 'x': x, 'attn_W': attn_W, 'attn_b': attn_b}
    _L0_rec_all = _L0_rec_setup()
    _L0_rec_in = {k: v for k, v in _L0_rec_all.items() if k in ('attn_W', 'attn_b')}
    del _L0_rec_all
    return {'r_gnn_feature': r_gnn_feature, 'ids': ids, 'tbl_0': tbl_0, 'tbl_1': tbl_1, 'tbl_2': tbl_2, 'tbl_3': tbl_3, 'tbl_4': tbl_4, 'tbl_5': tbl_5, 'tbl_6': tbl_6, 'tbl_7': tbl_7, 'tbl_8': tbl_8, 'tbl_9': tbl_9, 'tbl_10': tbl_10, 'tbl_11': tbl_11, 'tbl_12': tbl_12, 'tbl_13': tbl_13, 'tbl_14': tbl_14, 'tbl_15': tbl_15, 'tbl_16': tbl_16, 'tbl_17': tbl_17, 'tbl_18': tbl_18, 'tbl_19': tbl_19, 'tbl_20': tbl_20, 'tbl_21': tbl_21, 'tbl_22': tbl_22, 'tbl_23': tbl_23, 'tbl_24': tbl_24, 'tbl_25': tbl_25, 'tbl_26': tbl_26, 'tbl_27': tbl_27, 'tbl_28': tbl_28, 'tbl_29': tbl_29, 'tbl_30': tbl_30, 'tbl_31': tbl_31, 'tbl_32': tbl_32, 'W_top1': W_top1, 'b_top1': b_top1, 'W_top2': W_top2, 'b_top2': b_top2, 'W_top3': W_top3, 'L0_rec_attn_W': _L0_rec_in['attn_W'], 'L0_rec_attn_b': _L0_rec_in['attn_b']}

def reference(r_gnn_feature, ids, tbl_0, tbl_1, tbl_2, tbl_3, tbl_4, tbl_5, tbl_6, tbl_7, tbl_8, tbl_9, tbl_10, tbl_11, tbl_12, tbl_13, tbl_14, tbl_15, tbl_16, tbl_17, tbl_18, tbl_19, tbl_20, tbl_21, tbl_22, tbl_23, tbl_24, tbl_25, tbl_26, tbl_27, tbl_28, tbl_29, tbl_30, tbl_31, tbl_32, W_top1, b_top1, W_top2, b_top2, W_top3, L0_rec_attn_W, L0_rec_attn_b):
    import jax
    import jax.numpy as jnp

    def _L0_rec_ref(gnn_feature, x, attn_W, attn_b):
        import jax, jax.numpy as jnp
        import numpy as np
        B, F, D, A = (1024, 33, 128, 128)
        num_fields = x.shape[1]
        row, col = np.triu_indices(num_fields, k=1)
        inner = x[:, row] * x[:, col]
        fm = jax.nn.relu(jnp.einsum('bpd,ad->bpa', inner, attn_W) + attn_b)
        scores = jnp.einsum('ba,bpa->bp', gnn_feature, fm)
        attn = jax.nn.softmax(scores, axis=1)
        attn_output = jnp.einsum('bp,bpd->bd', attn, inner) * 100.0
        return jnp.concatenate([gnn_feature, attn_output], axis=1)
    e = jnp.stack([tbl_0[ids[:, 0]], tbl_1[ids[:, 1]], tbl_2[ids[:, 2]], tbl_3[ids[:, 3]], tbl_4[ids[:, 4]], tbl_5[ids[:, 5]], tbl_6[ids[:, 6]], tbl_7[ids[:, 7]], tbl_8[ids[:, 8]], tbl_9[ids[:, 9]], tbl_10[ids[:, 10]], tbl_11[ids[:, 11]], tbl_12[ids[:, 12]], tbl_13[ids[:, 13]], tbl_14[ids[:, 14]], tbl_15[ids[:, 15]], tbl_16[ids[:, 16]], tbl_17[ids[:, 17]], tbl_18[ids[:, 18]], tbl_19[ids[:, 19]], tbl_20[ids[:, 20]], tbl_21[ids[:, 21]], tbl_22[ids[:, 22]], tbl_23[ids[:, 23]], tbl_24[ids[:, 24]], tbl_25[ids[:, 25]], tbl_26[ids[:, 26]], tbl_27[ids[:, 27]], tbl_28[ids[:, 28]], tbl_29[ids[:, 29]], tbl_30[ids[:, 30]], tbl_31[ids[:, 31]], tbl_32[ids[:, 32]]], axis=1)
    z = _L0_rec_ref(r_gnn_feature, e, L0_rec_attn_W, L0_rec_attn_b)
    z = z.reshape(z.shape[0], -1)
    h = jnp.concatenate([z, r_gnn_feature], axis=1)
    h = jnp.maximum(h @ W_top1 + b_top1, 0.0)
    h = jnp.maximum(h @ W_top2 + b_top2, 0.0)
    y = h @ W_top3
    return y

_drawn_inputs = setup_inputs


def setup_inputs(seed=0):
    import zlib

    import numpy as np

    out = dict(_drawn_inputs(seed))
    spreads = {'b_top1': (0.0, 0.5), 'b_top2': (0.0, 0.1)}
    factors = {'tbl_0': 8.0,
     'tbl_1': 8.0,
     'tbl_2': 8.0,
     'tbl_3': 8.0,
     'tbl_4': 8.0,
     'tbl_5': 8.0,
     'tbl_6': 8.0,
     'tbl_7': 8.0,
     'tbl_8': 8.0,
     'tbl_9': 8.0,
     'tbl_10': 8.0,
     'tbl_11': 8.0,
     'tbl_12': 8.0,
     'tbl_13': 8.0,
     'tbl_14': 8.0,
     'tbl_15': 8.0,
     'tbl_16': 8.0,
     'tbl_17': 8.0,
     'tbl_18': 8.0,
     'tbl_19': 8.0,
     'tbl_20': 8.0,
     'tbl_21': 8.0,
     'tbl_22': 8.0,
     'tbl_23': 8.0,
     'tbl_24': 8.0,
     'tbl_25': 8.0,
     'tbl_26': 8.0,
     'tbl_27': 8.0,
     'tbl_28': 8.0,
     'tbl_29': 8.0,
     'tbl_30': 8.0,
     'tbl_31': 8.0,
     'tbl_32': 8.0,
     'L0_rec_attn_W': 8.0,
     'L0_rec_attn_b': 8.0}
    for name, (base, spread) in spreads.items():
        noise = np.random.default_rng([zlib.crc32(name.encode()), seed]).standard_normal(out[name].shape)
        drawn = base * np.exp(spread * noise) if base else spread * noise
        out[name] = jnp.asarray(drawn.astype(out[name].dtype))
    for name, factor in factors.items():
        out[name] = (out[name] * factor).astype(out[name].dtype)
    return out
```

```python
from contextlib import ExitStack

import numpy as np

import concourse.bass as bass
from concourse import mybir

BATCH = 512
FIELDS = 33
DIM = 128
TILE = 128
TILES = BATCH // TILE
SHIFTS = FIELDS // 2
PAIRS = SHIFTS * FIELDS
WIDE = FIELDS + SHIFTS
QUAD = 4
QUADS = TILE // QUAD
BODIES = QUADS // 2
DIRECT = 6
SPLIT = SHIFTS - DIRECT
DCOLS = DIRECT * FIELDS
SCOLS = SPLIT * FIELDS
HALF = PAIRS // 2
BANK = 512
GROUPS = 8
YPAIRS = 8
YCOLS = 2 * FIELDS
SQUARE = FIELDS * FIELDS
FIRST_SIDE = 5
LAST_SIDE = FIRST_SIDE + GROUPS
XFIELDS = 4
PRO = 10
SIDE = 2 * GROUPS + 2
HID1 = 512
HID2 = 256


def field_attention_tower(nc, gnn, ids, tables, w1, b1, w2, b2, w3, attn_w, attn_b, out):
    f32 = mybir.dt.float32
    f32r = mybir.dt.float32r
    ALU = mybir.AluOpType
    ACT = mybir.ActivationFunctionType
    AX = mybir.AxisListType.X
    AP = bass.AP

    rows_dram = nc.dram_tensor("rows_scratch", (TILES, TILE, FIELDS * DIM), f32)
    square_dram = nc.dram_tensor("square_scratch", (TILES, TILE, SQUARE), f32)

    with ExitStack() as ctx:
        def sb(name, shape, dt=f32):
            return ctx.enter_context(nc.sbuf_tensor(name, shape, dt))

        def sem(name):
            return ctx.enter_context(nc.semaphore(name))

        ids_sb = sb("ids_sb", [128, TILES, FIELDS], mybir.dt.int32)
        rows = sb("rows", [128, FIELDS, DIM])
        stage = sb("stage", [128, XFIELDS * DIM])
        emb = [sb(f"emb{i}", [128, TILE * WIDE]) for i in range(3)]
        prod_d = sb("prod_d", [128, 2, QUAD * DCOLS])
        prod_s = sb("prod_s", [128, 2, QUAD * SCOLS])
        high = sb("high", [128, 2, QUAD * SCOLS], f32r)
        low = sb("low", [128, 2, QUAD * SCOLS], f32r)
        fm = sb("fm", [128, 2, QUAD * PAIRS])
        gnn_sb = sb("gnn_sb", [128, TILES, DIM])
        gT = sb("gT", [128, BATCH])
        diag = [sb(f"diag{i}", [128, QUADS * QUAD * 32]) for i in range(2)]
        pick = sb("pick", [128, 2, QUAD * 32])
        wn = sb("wn", [128, DIM])
        wT = sb("wT", [128, 128])
        w_hi = sb("w_hi", [128, 128], f32r)
        w_lo = sb("w_lo", [128, 128], f32r)
        ident = sb("ident", [128, 128])
        attn_b_sb = sb("attn_b_sb", [128, 1])
        scores = sb("scores", [128, PAIRS])
        expd = sb("expd", [128, PAIRS])
        neg_max = sb("neg_max", [128, 1])
        total = sb("total", [128, 1])
        inv_total = sb("inv_total", [128, 1])
        square = sb("square", [128, WIDE * FIELDS])
        folded = expd
        yrows = sb("yrows", [2 * FIELDS, YPAIRS, DIM])
        ymat = sb("ymat", [2 * FIELDS, YPAIRS, YCOLS])
        ytmp = sb("ytmp", [128, 2, YPAIRS * FIELDS])
        z_raw = sb("z_raw", [128, BATCH])
        w3_sb = sb("w3_sb", [128, 2])
        b1_sb = sb("b1_sb", [128, 4])
        b2_sb = sb("b2_sb", [128, 2])
        zT = scores[:, 0:BATCH]
        w1_sb = diag[0][:, 0:3 * HID1].rearrange("p (c n) -> p c n", c=3)
        w2_sb = diag[0][:, 3 * HID1:3 * HID1 + 4 * HID2].rearrange("p (c n) -> p c n", c=4)
        h1 = fm[:, :, :].rearrange("p a n -> p (a n)")[:, 0:4 * BATCH]
        h2 = fm[:, :, :].rearrange("p a n -> p (a n)")[:, 4 * BATCH:6 * BATCH]
        y_sb = ytmp[0:1, :, :].rearrange("p h n -> p (h n)")[:, 0:BATCH]

        ps = ctx.enter_context(nc.psum_tensor("ps", [128, 4, BANK], f32))
        ps_sc = ctx.enter_context(nc.psum_tensor("ps_sc", [128, 2, BANK], f32))
        ps_y = ctx.enter_context(nc.psum_tensor("ps_y", [128, 2, BANK], f32))

        s_ids = sem("s_ids")
        s_wload = sem("s_wload")
        s_mlpload = sem("s_mlpload")
        s_ident = sem("s_ident")
        s_zero = sem("s_zero")
        s_field = [sem(f"s_field{i}") for i in range(9)]
        s_gather = sem("s_gather")
        s_rows_out = sem("s_rows_out")
        s_stage = sem("s_stage")
        s_emb = sem("s_emb")
        s_diag = sem("s_diag")
        s_pick = [sem("s_pick0"), sem("s_pick1")]
        s_split_w = sem("s_split_w")
        s_prod_d = sem("s_prod_d")
        s_prod_s = sem("s_prod_s")
        s_high = sem("s_high")
        s_low = sem("s_low")
        s_main = sem("s_main")
        s_relu = sem("s_relu")
        s_xpose = sem("s_xpose")
        s_copied = sem("s_copied")
        s_scores = sem("s_scores")
        s_sc_out = sem("s_sc_out")
        s_max = sem("s_max")
        s_exp = sem("s_exp")
        s_inv = sem("s_inv")
        s_band = sem("s_band")
        s_square = sem("s_square")
        s_square_out = sem("s_square_out")
        s_ylo = sem("s_ylo")
        s_y = sem("s_y")
        s_ymul = sem("s_ymul")
        s_z = sem("s_z")
        s_mlp = sem("s_mlp")
        s_mlpact = sem("s_mlpact")
        s_out = sem("s_out")

        def segments():
            for t in range(TILES):
                for k, n in ((0, 1), (1, 1), (2, 1), (3, 1), (4, 1), (FIRST_SIDE, 1), (FIRST_SIDE + 1, 1), (FIRST_SIDE + 2, GROUPS - 2),
                             (LAST_SIDE, 1), (LAST_SIDE + 1, 1), (LAST_SIDE + 2, 1)):
                    yield t, k, n

        def run(eng, body):
            for t, k, n in segments():
                if n == 1:
                    body(t, k, k)
                else:
                    with eng.Fori(0, n) as i:
                        body(t, k + i, k)

        def wait(eng, s, v):
            if not isinstance(v, int) or v > 0:
                eng.wait_ge(s, v)

        def side_x(t, k0):
            return t < TILES - 1 and FIRST_SIDE <= k0 <= LAST_SIDE

        def side_y(t, k0):
            return t > 0 and FIRST_SIDE <= k0 < LAST_SIDE

        block = ctx.enter_context(nc.Block())

        @block.sync
        def _(sp):
            sp.dma_start(ids_sb[:, :, :], ids.rearrange("(t p) f -> p t f", p=128)).then_inc(s_ids, 16)
            sp.dma_start(wn[:, :], attn_w).then_inc(s_wload, 16)
            sp.dma_start(gnn_sb[:, :, :], gnn.rearrange("(t p) a -> p t a", p=128)).then_inc(s_wload, 16)
            sp.dma_start(attn_b_sb[:, :], attn_b.rearrange("(a o) -> a o", o=1)).then_inc(s_wload, 16)
            with nc.allow_non_contiguous_dma(reason="a few hundred words of biases and output weights"):
                sp.dma_start(w3_sb[:, :], w3.rearrange("(c p) o -> p (c o)", p=128)).then_inc(s_mlpload, 16)
                sp.dma_start(b1_sb[:, :], b1.rearrange("(c p) -> p c", p=128)).then_inc(s_mlpload, 16)
                sp.dma_start(b2_sb[:, :], b2.rearrange("(c p) -> p c", p=128)).then_inc(s_mlpload, 16)

            def pick_load(t, k, q):
                sp.wait_ge(s_diag, t + 1)
                wait(sp, s_scores, 2 * (BODIES * t + k) + q - 1)
                sp.dma_start(pick[:, q, :], diag[t % 2][:, bass.ds((2 * k + q) * 128, 128)]).then_inc(s_pick[q], 16)

            def side_loads(t, g):
                wait(sp, s_y, 2 * (GROUPS * t + g))
                for r in range(2):
                    lane = slice(FIELDS * r, FIELDS * (r + 1))
                    src = AP(tensor=rows_dram, offset=t * TILE * FIELDS * DIM + (16 * g + r) * FIELDS * DIM,
                             ap=[[DIM, FIELDS], [2 * FIELDS * DIM, YPAIRS], [1, DIM]])
                    sp.dma_start(yrows[lane, :, :], src).then_inc(s_ylo, 16)
                    src = AP(tensor=square_dram, offset=t * TILE * SQUARE + (16 * g + r) * SQUARE,
                             ap=[[FIELDS, FIELDS], [2 * SQUARE, YPAIRS], [1, FIELDS]])
                    sp.dma_start(ymat[lane, :, lane], src).then_inc(s_ylo, 16)

            def body(t, k, k0):
                pick_load(t, k, 0)
                pick_load(t, k, 1)
                if FIRST_SIDE - 1 <= k0 < LAST_SIDE and t < TILES - 1:
                    if k0 == FIRST_SIDE - 1:
                        sp.wait_ge(s_gather, 16 * FIELDS * (t + 1))
                    sp.wait_ge(s_xpose, PRO + SIDE * t + 2 * (k - FIRST_SIDE + 1))
                    if k0 == LAST_SIDE - 1:
                        sp.dma_start(stage[:, 0:DIM], rows[:, FIELDS - 1, :]).then_inc(s_stage, 16)
                    else:
                        sp.dma_start(stage[:, :], rows[:, bass.ds(XFIELDS * (k - FIRST_SIDE + 1), XFIELDS), :]
                                     .rearrange("p f d -> p (f d)")).then_inc(s_stage, 16)
                if FIRST_SIDE - 1 <= k0 < LAST_SIDE - 1 and t > 0:
                    if k0 == FIRST_SIDE - 1:
                        sp.wait_ge(s_rows_out, 16 * t)
                        sp.wait_ge(s_square_out, 32 * t)
                    side_loads(t - 1, k - FIRST_SIDE + 1)

            for t in range(TILES):
                for k in range(FIRST_SIDE):
                    body(t, k, k)
                if t == TILES - 1:
                    for q in range(2):
                        sp.wait_ge(s_pick[q], 16 * BODIES * t)
                    sp.dma_start(w1_sb, w1.rearrange("(c p) n -> p c n", p=128)).then_inc(s_mlpload, 16)
                    sp.dma_start(w2_sb, w2.rearrange("(c p) n -> p c n", p=128)).then_inc(s_mlpload, 16)
                with sp.Fori(FIRST_SIDE, LAST_SIDE - 1) as k:
                    body(t, k, FIRST_SIDE)
                for k in range(LAST_SIDE - 1, BODIES):
                    body(t, k, k)
            sp.wait_ge(s_rows_out, 16 * TILES)
            sp.wait_ge(s_square_out, 32 * TILES)
            with sp.Fori(0, GROUPS) as g:
                side_loads(TILES - 1, g)
            sp.wait_ge(s_mlpact, 8)
            sp.dma_start(out.rearrange("b o -> o b"), y_sb).then_inc(s_out, 16)
            sp.wait_ge(s_out, 16)

        @block.gpsimd
        def _(pool):
            pool.memset(ident[:, :], 0.0).then_inc(s_ident, 1)
            pool.wait_ge(s_ident, 1)
            pool.affine_select(out=ident[:, :], in_=ident[:, :], compare_op=ALU.not_equal, fill=1.0,
                               base=0, pattern=[[-1, 128]], channel_multiplier=1).then_inc(s_ident, 1)

            def gather(t, f):
                return pool.indirect_dma_start(
                    out=rows[:, f, :], out_offset=None, in_=tables[f],
                    in_offset=bass.IndirectOffsetOnAxis(ap=ids_sb[:, t, f:f + 1], axis=0))

            def store_square(t):
                pool.wait_ge(s_square, t + 1)
                dst = square_dram[t].rearrange("b (j i) -> b (j i)", i=FIELDS)
                pool.dma_start(dst[:, 0:SHIFTS * FIELDS], folded[:, :]).then_inc(s_square_out, 16)
                pool.dma_start(dst[:, SHIFTS * FIELDS:], square[:, SHIFTS * FIELDS:SQUARE]).then_inc(s_square_out, 16)

            pool.wait_ge(s_ids, 16)
            for f in range(FIELDS):
                gather(0, f).then_inc(s_field[f // XFIELDS], 16)
            for i, s in enumerate(s_field):
                pool.wait_ge(s, 16 * min(XFIELDS, FIELDS - XFIELDS * i))
            pool.dma_start(rows_dram[0], rows[:, :, :].rearrange("p f d -> p (f d)")).then_inc(s_rows_out, 16)
            for t in range(1, TILES):
                pool.wait_ge(s_rows_out, 16 * t)
                if t == 1:
                    pool.wait_ge(s_xpose, PRO)
                else:
                    pool.wait_ge(s_stage, 16 * (GROUPS + 1) * (t - 1))
                for f in range(FIELDS):
                    gather(t, f).then_inc(s_gather, 16)
                pool.wait_ge(s_gather, 16 * FIELDS * t)
                pool.dma_start(rows_dram[t], rows[:, :, :].rearrange("p f d -> p (f d)")).then_inc(s_rows_out, 16)
                if t >= 2:
                    store_square(t - 2)
            store_square(TILES - 2)
            store_square(TILES - 1)

        @block.vector
        def _(dve):
            nc.vector.memset(diag[0][:, :], 0.0).then_inc(s_zero, 1)
            nc.vector.memset(diag[1][:, :], 0.0).then_inc(s_zero, 1)
            nc.vector.memset(square[:, :], 0.0).then_inc(s_zero, 1)
            nc.vector.memset(ymat[:, :, :], 0.0).then_inc(s_zero, 1)
            dve.wait_ge(s_split_w, 2)
            nc.vector.tensor_tensor(w_lo[:, :], wT[:, :], w_hi[:, :], ALU.subtract).then_inc(s_split_w, 1)

            def products(dst, t, k, q, first, count):
                e, row = emb[t % 3], TILE * WIDE
                at = (2 * k + q) * WIDE
                a = AP(tensor=e, offset=at, ap=[[row, 128], [32 * WIDE, QUAD], [0, count], [1, FIELDS]])
                b = AP(tensor=e, offset=at + first, ap=[[row, 128], [32 * WIDE, QUAD], [1, count], [1, FIELDS]])
                o = dst.rearrange("p (g s i) -> p g s i", g=QUAD, i=FIELDS)
                return nc.vector.tensor_tensor(o, a, b, ALU.mult)

            def low_half(n, q):
                wait(dve, s_prod_s, n + 1)
                wait(dve, s_high, n + 1)
                wait(dve, s_main, 3 * (n - 1))
                nc.vector.tensor_tensor(low[:, q, :], prod_s[:, q, :], high[:, q, :],
                                        ALU.subtract).then_inc(s_low, 1)

            def y_half(t, g, h):
                at = 2 * (GROUPS * t + g) + h
                dve.wait_ge(s_y, at + 1)
                wait(dve, s_z, at - 1)
                e = AP(tensor=emb[t % 3], offset=(16 * g + 8 * h) * WIDE,
                       ap=[[TILE * WIDE, 128], [WIDE, 8], [1, FIELDS]])
                nc.vector.tensor_tensor(ytmp[:, h, :].rearrange("p (b i) -> p b i", i=FIELDS), e,
                                        ps_y[:, h, 0:8 * FIELDS].rearrange("p (b i) -> p b i", i=FIELDS),
                                        ALU.mult).then_inc(s_ymul, 1)
                dve.wait_ge(s_ymul, at + 1)
                nc.vector.tensor_reduce(z_raw[:, bass.ds(TILE * t + 16 * g + 8 * h, 8)],
                                        ytmp[:, h, :].rearrange("p (b i) -> p b i", i=FIELDS),
                                        axis=AX, op=ALU.add).then_inc(s_z, 1)

            def softmax_max(t):
                dve.wait_ge(s_sc_out, t + 1)
                nc.vector.tensor_reduce(neg_max[:, :], scores[:, :], axis=AX, op=ALU.max,
                                        negate=True).then_inc(s_max, 1)

            def softmax_scale(t):
                dve.wait_ge(s_exp, t + 1)
                nc.vector.reciprocal(inv_total[:, :], total[:, :]).then_inc(s_inv, 1)
                dve.wait_ge(s_inv, t + 1)
                wait(dve, s_square_out, 32 * t)
                band = AP(tensor=square, offset=FIELDS,
                          ap=[[WIDE * FIELDS, 128], [FIELDS, SHIFTS], [FIELDS + 1, FIELDS]])
                nc.vector.tensor_scalar(band, expd[:, :].rearrange("p (s i) -> p s i", i=FIELDS),
                                        inv_total[:, 0:1], None, ALU.mult).then_inc(s_band, 1)
                dve.wait_ge(s_band, t + 1)
                nc.vector.tensor_tensor(folded[:, :], square[:, 0:SHIFTS * FIELDS],
                                        square[:, SQUARE:SQUARE + SHIFTS * FIELDS], ALU.add).then_inc(s_square, 1)

            def body(t, k, k0):
                if k0 == 0:
                    dve.wait_ge(s_emb, t + 1)
                if t > 0 and k0 == 2:
                    softmax_max(t - 1)
                if t > 0 and k0 == 3:
                    softmax_scale(t - 1)
                for q in range(2):
                    n = 2 * (BODIES * t + k) + q
                    wait(dve, s_low, n - 1)
                    products(prod_s[:, q, :], t, k, q, DIRECT + 1, SPLIT).then_inc(s_prod_s, 1)
                    if t > 0 or k0 > 0 or q > 0:
                        low_half(n - 1, 1 - q)
                    wait(dve, s_main, 3 * (n - 2) + 1)
                    products(prod_d[:, q, :], t, k, q, 1, DIRECT).then_inc(s_prod_d, 1)
                    if t > 0 and FIRST_SIDE < k0 <= LAST_SIDE:
                        y_half(t - 1, k - FIRST_SIDE - 1, q)

            dve.wait_ge(s_zero, 4)
            run(dve, body)
            low_half(2 * BODIES * TILES - 1, 1)
            softmax_max(TILES - 1)
            softmax_scale(TILES - 1)
            with dve.Fori(0, GROUPS) as g:
                y_half(TILES - 1, g, 0)
                y_half(TILES - 1, g, 1)

        @block.scalar
        def _(act):
            def emb_copy(e, f, n, src):
                dst = AP(tensor=e, offset=f, ap=[[TILE * WIDE, 128], [1, n], [WIDE, TILE]])
                return nc.scalar.activation(dst, src.rearrange("p (f b) -> p f b", b=TILE), ACT.Copy)

            def emb_finish(t, copied):
                act.wait_ge(s_copied, copied)
                v = emb[t % 3][:, :].rearrange("p (b f) -> p b f", f=WIDE)
                nc.scalar.activation(v[:, :, FIELDS:WIDE], v[:, :, 0:SHIFTS], ACT.Copy).then_inc(s_emb, 1)

            def make_diag(t, copied):
                act.wait_ge(s_copied, copied)
                if t >= 2:
                    for q in range(2):
                        act.wait_ge(s_pick[q], 16 * BODIES * (t - 1))
                dst = AP(tensor=diag[t % 2], offset=0, ap=[[QUADS * 128, 128], [129, QUADS], [32, QUAD]])
                src = AP(tensor=gT, offset=TILE * t, ap=[[BATCH, 128], [1, QUADS], [32, QUAD]])
                nc.scalar.activation(dst, src, ACT.Copy).then_inc(s_diag, 1)

            act.wait_ge(s_xpose, 1)
            nc.scalar.activation(wT[:, :], ps[:, 0, 0:128], ACT.Copy).then_inc(s_split_w, 1)
            nc.scalar.activation(gT[:, 0:TILE], ps[:, 0, 128:256], ACT.Copy).then_inc(s_copied, 1)
            act.wait_ge(s_split_w, 1)
            nc.scalar.activation(w_hi[:, :], wT[:, :], ACT.Copy).then_inc(s_split_w, 1)
            act.wait_ge(s_zero, 4)
            make_diag(0, 1)
            for v in range(1, PRO):
                f, n = XFIELDS * (v - 1), min(XFIELDS, FIELDS - XFIELDS * (v - 1))
                act.wait_ge(s_xpose, v + 1)
                emb_copy(emb[0], f, n, ps[:, 2 * (v % 2), 0:n * TILE]).then_inc(s_copied, 1)
            emb_finish(0, PRO)
            act.wait_ge(s_wload, 48)

            def relu(n, q, j, slot):
                act.wait_ge(s_main, 3 * n + j + 1)
                if j == 0:
                    wait(act, s_scores, n - 1)
                if j == 0:
                    dst = AP(tensor=fm, offset=q * QUAD * PAIRS,
                             ap=[[2 * QUAD * PAIRS, 128], [2 * PAIRS, 2], [PAIRS, 2], [1, DCOLS]])
                    src = ps[:, 2 * slot:2 * slot + 2, 0:2 * DCOLS].rearrange("p c (g n) -> p c g n", g=2)
                else:
                    dst = AP(tensor=fm, offset=q * QUAD * PAIRS + 2 * (j - 1) * PAIRS + DCOLS,
                             ap=[[2 * QUAD * PAIRS, 128], [PAIRS, 2], [1, SCOLS]])
                    src = ps[:, 2 * slot:2 * slot + 2, 0:SCOLS]
                nc.scalar.activation(dst, src, ACT.Relu, bias=attn_b_sb[:, 0:1]).then_inc(s_relu, 1)

            def high_half(n, q):
                act.wait_ge(s_prod_s, n + 1)
                wait(act, s_main, 3 * (n - 1))
                wait(act, s_low, n - 1)
                nc.scalar.activation(high[:, q, :], prod_s[:, q, :], ACT.Copy).then_inc(s_high, 1)

            def scores_out(t):
                act.wait_ge(s_scores, QUADS * (t + 1))
                wait(act, s_exp, t)
                nc.scalar.activation(scores[:, :].rearrange("p (c n) -> p c n", c=2), ps_sc[:, :, 0:HALF],
                                     ACT.Copy).then_inc(s_sc_out, 1)

            def exponentials(t):
                act.wait_ge(s_max, t + 1)
                wait(act, s_square_out, 32 * t)
                nc.scalar.activation(expd[:, :], scores[:, :], ACT.Exp, bias=neg_max[:, 0:1],
                                     accum_out=total[:, 0:1]).then_inc(s_exp, 1)

            def drain_quad(t, k, k0, q):
                n = 2 * (BODIES * t + k) + q
                x = side_x(t, k0)
                for j in range(3):
                    relu(n, q, j, j % 2 if x else (3 * q + j) % 2)
                if x:
                    v = PRO + SIDE * t + 2 * (k - FIRST_SIDE) + q
                    act.wait_ge(s_xpose, v + 1)
                    if k0 < LAST_SIDE:
                        emb_copy(emb[(t + 1) % 3], XFIELDS * (k - FIRST_SIDE) + 2 * q, 2,
                                 ps[:, 2, 0:2 * TILE]).then_inc(s_copied, 1)
                    elif q == 0:
                        emb_copy(emb[(t + 1) % 3], FIELDS - 1, 1, ps[:, 2, 0:TILE]).then_inc(s_copied, 1)
                        emb_finish(t + 1, v + 1)
                    else:
                        nc.scalar.activation(gT[:, TILE * (t + 1):TILE * (t + 2)], ps[:, 2, 0:TILE],
                                             ACT.Copy).then_inc(s_copied, 1)
                        make_diag(t + 1, v + 1)

            def body(t, k, k0, dt, dk, dk0):
                for q in range(2):
                    if dt >= 0:
                        drain_quad(dt, dk, dk0, q)
                    if q == 0 and t > 0 and k0 == 1:
                        scores_out(t - 1)
                    high_half(2 * (BODIES * t + k) + q, q)
                if t > 0 and k0 == 2:
                    exponentials(t - 1)

            for t, k, n in segments():
                if n == 1:
                    body(t, k, k, t if k else t - 1, (k - 1) % BODIES, (k - 1) % BODIES)
                else:
                    with act.Fori(0, n) as i:
                        body(t, k + i, k, t, k - 1 + i, k - 1)
            drain_quad(TILES - 1, BODIES - 1, BODIES - 1, 0)
            drain_quad(TILES - 1, BODIES - 1, BODIES - 1, 1)
            scores_out(TILES - 1)
            exponentials(TILES - 1)
            act.wait_ge(s_z, 2 * GROUPS * TILES)
            nc.scalar.activation(zT[:, :], z_raw[:, :], ACT.Copy, scale=100.0).then_inc(s_mlpact, 1)
            act.wait_ge(s_mlpload, 80)
            for m in range(4):
                act.wait_ge(s_mlp, m + 1)
                nc.scalar.activation(h1[:, m * BATCH:(m + 1) * BATCH], ps[:, m, :], ACT.Relu,
                                     bias=b1_sb[:, m:m + 1]).then_inc(s_mlpact, 1)
            for m in range(2):
                act.wait_ge(s_mlp, 5 + m)
                nc.scalar.activation(h2[:, m * BATCH:(m + 1) * BATCH], ps_sc[:, m, :], ACT.Relu,
                                     bias=b2_sb[:, m:m + 1]).then_inc(s_mlpact, 1)
            act.wait_ge(s_mlp, 7)
            nc.scalar.activation(y_sb, ps_y[0:1, 0, :], ACT.Copy).then_inc(s_mlpact, 1)

        @block.tensor
        def _(pe):
            pe.wait_ge(s_ident, 2)
            pe.wait_ge(s_wload, 48)
            nc.tensor.transpose(ps[:, 0, 0:128], wn[:, :], ident[:, :])
            nc.tensor.transpose(ps[:, 0, 128:256], gnn_sb[:, 0, :], ident[:, :]).then_inc(s_xpose, 1)
            for v in range(1, PRO):
                f, n = XFIELDS * (v - 1), min(XFIELDS, FIELDS - XFIELDS * (v - 1))
                pe.wait_ge(s_field[v - 1], 16 * n)
                if v >= 2:
                    pe.wait_ge(s_copied, v - 1)
                for c in range(n):
                    last = nc.tensor.transpose(ps[:, 2 * (v % 2), c * TILE:(c + 1) * TILE],
                                               rows[:, f + c, :], ident[:, :])
                last.then_inc(s_xpose, 1)
            pe.wait_ge(s_split_w, 3)

            def multiply(t, k, k0, q):
                n = 2 * (BODIES * t + k) + q
                x = side_x(t, k0)
                for j in range(3):
                    m = 3 * n + j
                    slot = j % 2 if x else (3 * q + j) % 2
                    if j == 0:
                        pe.wait_ge(s_prod_d, n + 1)
                    if j == 1:
                        pe.wait_ge(s_low, n + 1)
                    if x and j == 0:
                        pe.wait_ge(s_relu, m)
                    elif x and j == 1:
                        pe.wait_ge(s_relu, m - 1)
                        pe.wait_ge(s_copied, PRO + SIDE * t + 2 * (k - FIRST_SIDE) + q)
                    elif k0 == LAST_SIDE + 1 and t < TILES - 1 and q == 0 and j < 2:
                        pe.wait_ge(s_relu, m if j == 0 else m - 1)
                        pe.wait_ge(s_copied, PRO + SIDE * (t + 1))
                    elif t == 0 and k0 == 0 and q == 0 and j < 2:
                        pe.wait_ge(s_copied, PRO)
                    else:
                        pe.wait_ge(s_relu, m - 1)
                    if j == 0:
                        for c in range(2):
                            last = nc.tensor.matmul(ps[:, 2 * slot + c, 0:2 * DCOLS], wT[:, :],
                                                    prod_d[:, q, c * 2 * DCOLS:(c + 1) * 2 * DCOLS],
                                                    start=True, stop=True)
                    else:
                        for a, (w, p) in enumerate(((w_hi, high), (w_hi, low), (w_lo, high))):
                            for c in range(2):
                                g = 2 * (j - 1) + c
                                last = nc.tensor.matmul(ps[:, 2 * slot + c, 0:SCOLS], w[:, :],
                                                        p[:, q, g * SCOLS:(g + 1) * SCOLS],
                                                        start=(a == 0), stop=(a == 2))
                    last.then_inc(s_main, 1)

            def transposes(t, k, k0, q):
                pe.wait_ge(s_relu, 3 * (2 * (BODIES * t + k) + q) + 2)
                if q == 0:
                    pe.wait_ge(s_stage, 16 * ((GROUPS + 1) * t + k - FIRST_SIDE + 1))
                if k0 < LAST_SIDE:
                    for c in range(2):
                        last = nc.tensor.transpose(ps[:, 2, c * TILE:(c + 1) * TILE],
                                                   stage[:, (2 * q + c) * DIM:(2 * q + c + 1) * DIM], ident[:, :])
                elif q == 0:
                    last = nc.tensor.transpose(ps[:, 2, 0:TILE], stage[:, 0:DIM], ident[:, :])
                else:
                    last = nc.tensor.transpose(ps[:, 2, 0:TILE], gnn_sb[:, t + 1, :], ident[:, :])
                last.then_inc(s_xpose, 1)

            def score(n, q, first, last_quad):
                pe.wait_ge(s_relu, 3 * n + 3)
                for c in range(2):
                    for g in range(QUAD):
                        last = nc.tensor.matmul(ps_sc[32 * g:32 * g + 32, c, 0:HALF],
                                                pick[:, q, 32 * g:32 * g + 32],
                                                fm[:, q, g * PAIRS + c * HALF:g * PAIRS + (c + 1) * HALF],
                                                start=first, stop=last_quad)
                last.then_inc(s_scores, 1)

            def y_multiply(t, g, h):
                at = 2 * (GROUPS * t + g) + h
                if h == 0:
                    pe.wait_ge(s_ylo, 64 * (GROUPS * t + g + 1))
                wait(pe, s_ymul, at - 1)
                for m in range(YPAIRS // 2):
                    last = nc.tensor.matmul(ps_y[:, h, m * YCOLS:(m + 1) * YCOLS], yrows[:, YPAIRS // 2 * h + m, :],
                                            ymat[:, YPAIRS // 2 * h + m, :], start=True, stop=True)
                last.then_inc(s_y, 1)

            def body(t, k, k0):
                for q in range(2):
                    n = 2 * (BODIES * t + k) + q
                    multiply(t, k, k0, q)
                    if side_x(t, k0):
                        transposes(t, k, k0, q)
                    if t > 0 or k0 > 0 or q > 0:
                        pe.wait_ge(s_pick[1 - q], 16 * (BODIES * t + k + q))
                        first = k0 == 0 and q == 1
                        if first and t > 0:
                            pe.wait_ge(s_sc_out, t)
                        score(n - 1, 1 - q, first, k0 == 0 and q == 0)
                    if side_y(t, k0):
                        y_multiply(t - 1, k - FIRST_SIDE, q)

            run(pe, body)
            pe.wait_ge(s_pick[1], 16 * BODIES * TILES)
            score(2 * BODIES * TILES - 1, 1, False, True)
            with pe.Fori(0, GROUPS) as g:
                y_multiply(TILES - 1, g, 0)
                y_multiply(TILES - 1, g, 1)
            pe.wait_ge(s_mlpload, 80)
            pe.wait_ge(s_mlpact, 1)
            for m in range(4):
                for c, rhs in enumerate((gT, zT, gT)):
                    last = nc.tensor.matmul(ps[:, m, :], w1_sb[:, c, m * 128:(m + 1) * 128], rhs[:, :],
                                            start=(c == 0), stop=(c == 2))
                last.then_inc(s_mlp, 1)
            for m in range(2):
                pe.wait_ge(s_sc_out, TILES)
                for c in range(4):
                    pe.wait_ge(s_mlpact, 2 + c)
                    last = nc.tensor.matmul(ps_sc[:, m, :], w2_sb[:, c, m * 128:(m + 1) * 128],
                                            h1[:, c * BATCH:(c + 1) * BATCH], start=(c == 0), stop=(c == 3))
                last.then_inc(s_mlp, 1)
            pe.wait_ge(s_ymul, 2 * GROUPS * TILES)
            for c in range(2):
                pe.wait_ge(s_mlpact, 6 + c)
                last = nc.tensor.matmul(ps_y[0:1, 0, :], w3_sb[:, c:c + 1], h2[:, c * BATCH:(c + 1) * BATCH],
                                        start=(c == 0), stop=(c == 1))
            last.then_inc(s_mlp, 1)


def kernel(**inputs):
    import numpy as _np
    import concourse.bacc as _bacc
    from concourse import mybir as _mybir
    from concourse.bass_utils import run_bass_kernel_spmd as _run

    nc = _bacc.Bacc("TRN2", target_bir_lowering=False, num_devices=1)
    arrays, aps = {}, {}
    for name, value in inputs.items():
        a = _np.ascontiguousarray(value)
        arrays[f"in_{name}_dram"] = a
        aps[name] = nc.dram_tensor(f"in_{name}_dram", a.shape, _mybir.dt.from_np(a.dtype), kind="ExternalInput").ap()
    out = nc.dram_tensor("out_0_dram", (BATCH, 1), _mybir.dt.float32, kind="ExternalOutput").ap()
    field_attention_tower(nc, aps["r_gnn_feature"], aps["ids"], [aps[f"tbl_{f}"] for f in range(FIELDS)],
                          aps["W_top1"], aps["b_top1"], aps["W_top2"], aps["b_top2"], aps["W_top3"],
                          aps["L0_rec_attn_W"], aps["L0_rec_attn_b"], out)
    r = _run(nc, [arrays], core_ids=[0])
    return r.results[0]["out_0_dram"]
```

```python
from contextlib import ExitStack

import numpy as np

import concourse.bass as bass
from concourse import mybir

BATCH = 512
FIELDS = 33
DIM = 128
TILE = 128
TILES = BATCH // TILE
SHIFTS = FIELDS // 2
PAIRS = SHIFTS * FIELDS
WIDE = FIELDS + SHIFTS
QUAD = 4
QUADS = TILE // QUAD
BODIES = QUADS // 2
DIRECT = 6
SPLIT = SHIFTS - DIRECT
DCOLS = DIRECT * FIELDS
SCOLS = SPLIT * FIELDS
HALF = PAIRS // 2
BANK = 512
GROUPS = 8
YPAIRS = 8
YCOLS = 2 * FIELDS
TPAIRS = TILE // 4
EARLY = BATCH - TILE
SQUARE = FIELDS * FIELDS
FIRST_SIDE = 5
LAST_SIDE = FIRST_SIDE + GROUPS
XFIELDS = 4
PRO = 10
SIDE = 2 * GROUPS + 2
HID1 = 512
HID2 = 256


def field_attention_tower(nc, gnn, ids, tables, w1, b1, w2, b2, w3, attn_w, attn_b, out):
    f32 = mybir.dt.float32
    f32r = mybir.dt.float32r
    ALU = mybir.AluOpType
    ACT = mybir.ActivationFunctionType
    AX = mybir.AxisListType.X
    AP = bass.AP

    rows_dram = nc.dram_tensor("rows_scratch", (TILES, TILE, FIELDS * DIM), f32)
    square_dram = nc.dram_tensor("square_scratch", (TILES, TILE, SQUARE), f32)

    with ExitStack() as ctx:
        def sb(name, shape, dt=f32):
            return ctx.enter_context(nc.sbuf_tensor(name, shape, dt))

        def sem(name):
            return ctx.enter_context(nc.semaphore(name))

        ids_sb = sb("ids_sb", [128, TILES, FIELDS], mybir.dt.int32)
        rows = sb("rows", [128, FIELDS, DIM])
        stage = sb("stage", [128, XFIELDS * DIM])
        emb = [sb(f"emb{i}", [128, TILE * WIDE]) for i in range(3)]
        prod_d = sb("prod_d", [128, 2, QUAD * DCOLS])
        prod_s = sb("prod_s", [128, 2, QUAD * SCOLS])
        high = sb("high", [128, 2, QUAD * SCOLS], f32r)
        low = sb("low", [128, 2, QUAD * SCOLS], f32r)
        fm = sb("fm", [128, 2, QUAD * PAIRS])
        gnn_sb = sb("gnn_sb", [128, TILES, DIM])
        gT = sb("gT", [128, BATCH])
        diag = [sb(f"diag{i}", [128, QUADS * QUAD * 32]) for i in range(2)]
        pick = sb("pick", [128, 2, QUAD * 32])
        wn = sb("wn", [128, DIM])
        wT = sb("wT", [128, 128])
        w_hi = sb("w_hi", [128, 128], f32r)
        w_lo = sb("w_lo", [128, 128], f32r)
        ident = sb("ident", [128, 128])
        attn_b_sb = sb("attn_b_sb", [128, 1])
        scores = sb("scores", [128, PAIRS])
        expd = sb("expd", [128, PAIRS])
        neg_max = sb("neg_max", [128, 1])
        total = sb("total", [128, 1])
        inv_total = sb("inv_total", [128, 1])
        square = sb("square", [128, WIDE * FIELDS])
        folded = expd
        yrows = sb("yrows", [2 * FIELDS, YPAIRS, DIM])
        ymat = sb("ymat", [2 * FIELDS, YPAIRS, YCOLS])
        ytmp = sb("ytmp", [128, 2, YPAIRS * FIELDS])
        z_raw = sb("z_raw", [128, BATCH])
        w3_sb = sb("w3_sb", [128, 2])
        b1_sb = sb("b1_sb", [128, 4])
        b2_sb = sb("b2_sb", [128, 2])
        tail_rows = [v[0:2 * FIELDS, 0:TPAIRS * DIM].rearrange("p (m d) -> p m d", d=DIM)
                     for v in (rows[:, :, :].rearrange("p f d -> p (f d)"), emb[1])]
        tail_mat = emb[2][0:2 * FIELDS, 0:2 * TPAIRS * YCOLS].rearrange("p (m i) -> p m i", i=YCOLS)
        zT = emb[1][:, TPAIRS * DIM:TPAIRS * DIM + BATCH]
        w1_sb = diag[0][:, 0:3 * HID1].rearrange("p (c n) -> p c n", c=3)
        w2_sb = diag[0][:, 3 * HID1:3 * HID1 + 4 * HID2].rearrange("p (c n) -> p c n", c=4)
        h1 = fm[:, :, :].rearrange("p a n -> p (a n)")[:, 0:4 * BATCH]
        h2 = fm[:, :, :].rearrange("p a n -> p (a n)")[:, 4 * BATCH:6 * BATCH]
        y_sb = ytmp[0:1, :, :].rearrange("p h n -> p (h n)")[:, 0:BATCH]

        ps = ctx.enter_context(nc.psum_tensor("ps", [128, 4, BANK], f32))
        ps_sc = ctx.enter_context(nc.psum_tensor("ps_sc", [128, 2, BANK], f32))
        ps_y = ctx.enter_context(nc.psum_tensor("ps_y", [128, 2, BANK], f32))

        s_ids = sem("s_ids")
        s_wload = sem("s_wload")
        s_mlpload = sem("s_mlpload")
        s_ident = sem("s_ident")
        s_zero = sem("s_zero")
        s_field = [sem(f"s_field{i}") for i in range(9)]
        s_gather = sem("s_gather")
        s_rows_out = sem("s_rows_out")
        s_stage = sem("s_stage")
        s_emb = sem("s_emb")
        s_diag = sem("s_diag")
        s_pick = [sem("s_pick0"), sem("s_pick1")]
        s_split_w = sem("s_split_w")
        s_prod_d = sem("s_prod_d")
        s_prod_s = sem("s_prod_s")
        s_high = sem("s_high")
        s_low = sem("s_low")
        s_main = sem("s_main")
        s_relu = sem("s_relu")
        s_xpose = sem("s_xpose")
        s_copied = sem("s_copied")
        s_scores = sem("s_scores")
        s_sc_out = sem("s_sc_out")
        s_max = sem("s_max")
        s_exp = sem("s_exp")
        s_inv = sem("s_inv")
        s_band = sem("s_band")
        s_square = sem("s_square")
        s_square_out = sem("s_square_out")
        s_square_last = sem("s_square_last")
        s_ylo = sem("s_ylo")
        s_y = sem("s_y")
        s_ymul = sem("s_ymul")
        s_z = sem("s_z")
        s_tail_rows = sem("s_tail_rows")
        s_tail_zero = sem("s_tail_zero")
        s_tail_mat = sem("s_tail_mat")
        s_tail_y = sem("s_tail_y")
        s_tail_ymul = sem("s_tail_ymul")
        s_tail_z = sem("s_tail_z")
        s_mlp = sem("s_mlp")
        s_mlpact = sem("s_mlpact")
        s_out = sem("s_out")

        def segments():
            for t in range(TILES):
                for k, n in ((0, 1), (1, 1), (2, 1), (3, 1), (4, 1), (FIRST_SIDE, 1), (FIRST_SIDE + 1, 1), (FIRST_SIDE + 2, GROUPS - 2),
                             (LAST_SIDE, 1), (LAST_SIDE + 1, 1), (LAST_SIDE + 2, 1)):
                    yield t, k, n

        def run(eng, body):
            for t, k, n in segments():
                if n == 1:
                    body(t, k, k)
                else:
                    with eng.Fori(0, n) as i:
                        body(t, k + i, k)

        def wait(eng, s, v):
            if not isinstance(v, int) or v > 0:
                eng.wait_ge(s, v)

        def side_x(t, k0):
            return t < TILES - 1 and FIRST_SIDE <= k0 <= LAST_SIDE

        def side_y(t, k0):
            return t > 0 and FIRST_SIDE <= k0 < LAST_SIDE

        def store_square(eng, t, stored):
            dst = square_dram[t]
            eng.dma_start(dst[:, 0:SHIFTS * FIELDS], folded[:, :]).then_inc(stored, 16)
            eng.dma_start(dst[:, SHIFTS * FIELDS:SQUARE], square[:, SHIFTS * FIELDS:SQUARE]).then_inc(stored, 16)

        block = ctx.enter_context(nc.Block())

        @block.sync
        def _(sp):
            sp.dma_start(ids_sb[:, :, :], ids.rearrange("(t p) f -> p t f", p=128)).then_inc(s_ids, 16)
            sp.dma_start(wn[:, :], attn_w).then_inc(s_wload, 16)
            sp.dma_start(gnn_sb[:, :, :], gnn.rearrange("(t p) a -> p t a", p=128)).then_inc(s_wload, 16)
            sp.dma_start(attn_b_sb[:, :], attn_b.rearrange("(a o) -> a o", o=1)).then_inc(s_wload, 16)
            with nc.allow_non_contiguous_dma(reason="a few hundred words of biases and output weights"):
                sp.dma_start(w3_sb[:, :], w3.rearrange("(c p) o -> p (c o)", p=128)).then_inc(s_mlpload, 16)
                sp.dma_start(b1_sb[:, :], b1.rearrange("(c p) -> p c", p=128)).then_inc(s_mlpload, 16)
                sp.dma_start(b2_sb[:, :], b2.rearrange("(c p) -> p c", p=128)).then_inc(s_mlpload, 16)

            def pick_load(t, k, q):
                sp.wait_ge(s_diag, t + 1)
                wait(sp, s_scores, 2 * (BODIES * t + k) + q - 1)
                sp.dma_start(pick[:, q, :], diag[t % 2][:, bass.ds((2 * k + q) * 128, 128)]).then_inc(s_pick[q], 16)

            def side_loads(t, g):
                wait(sp, s_y, 2 * (GROUPS * t + g))
                for r in range(2):
                    lane = slice(FIELDS * r, FIELDS * (r + 1))
                    src = AP(tensor=rows_dram, offset=t * TILE * FIELDS * DIM + (16 * g + r) * FIELDS * DIM,
                             ap=[[DIM, FIELDS], [2 * FIELDS * DIM, YPAIRS], [1, DIM]])
                    sp.dma_start(yrows[lane, :, :], src).then_inc(s_ylo, 16)
                    src = AP(tensor=square_dram, offset=t * TILE * SQUARE + (16 * g + r) * SQUARE,
                             ap=[[FIELDS, FIELDS], [2 * SQUARE, YPAIRS], [1, FIELDS]])
                    sp.dma_start(ymat[lane, :, lane], src).then_inc(s_ylo, 16)

            def body(t, k, k0):
                pick_load(t, k, 0)
                pick_load(t, k, 1)
                if FIRST_SIDE - 1 <= k0 < LAST_SIDE and t < TILES - 1:
                    if k0 == FIRST_SIDE - 1:
                        sp.wait_ge(s_gather, 16 * FIELDS * (t + 1))
                    sp.wait_ge(s_xpose, PRO + SIDE * t + 2 * (k - FIRST_SIDE + 1))
                    if k0 == LAST_SIDE - 1:
                        sp.dma_start(stage[:, 0:DIM], rows[:, FIELDS - 1, :]).then_inc(s_stage, 16)
                    else:
                        sp.dma_start(stage[:, :], rows[:, bass.ds(XFIELDS * (k - FIRST_SIDE + 1), XFIELDS), :]
                                     .rearrange("p f d -> p (f d)")).then_inc(s_stage, 16)
                if FIRST_SIDE - 1 <= k0 < LAST_SIDE - 1 and t > 0:
                    if k0 == FIRST_SIDE - 1:
                        sp.wait_ge(s_rows_out, 16 * t)
                        sp.wait_ge(s_square_out, 32 * t)
                    side_loads(t - 1, k - FIRST_SIDE + 1)

            for t in range(TILES):
                for k in range(FIRST_SIDE):
                    body(t, k, k)
                if t == TILES - 1:
                    sp.wait_ge(s_rows_out, 16 * TILES)
                    sp.wait_ge(s_stage, 16 * (GROUPS + 1) * (TILES - 1))
                    sp.wait_ge(s_z, 2 * GROUPS * (TILES - 2))
                    for h in range(2):
                        for r in range(2):
                            src = AP(tensor=rows_dram, offset=(t * TILE + 2 * TPAIRS * h + r) * FIELDS * DIM,
                                     ap=[[DIM, FIELDS], [2 * FIELDS * DIM, TPAIRS], [1, DIM]])
                            sp.dma_start(tail_rows[h][FIELDS * r:FIELDS * (r + 1), :, :], src).then_inc(s_tail_rows, 16)
                    for q in range(2):
                        sp.wait_ge(s_pick[q], 16 * BODIES * t)
                    sp.dma_start(w1_sb, w1.rearrange("(c p) n -> p c n", p=128)).then_inc(s_mlpload, 16)
                    sp.dma_start(w2_sb, w2.rearrange("(c p) n -> p c n", p=128)).then_inc(s_mlpload, 16)
                with sp.Fori(FIRST_SIDE, LAST_SIDE - 1) as k:
                    body(t, k, FIRST_SIDE)
                for k in range(LAST_SIDE - 1, BODIES):
                    body(t, k, k)
            t = TILES - 1
            sp.wait_ge(s_square, TILES)
            store_square(sp, t, s_square_last)
            sp.wait_ge(s_square_last, 32)
            sp.wait_ge(s_tail_zero, 1)
            for r in range(2):
                lane = slice(FIELDS * r, FIELDS * (r + 1))
                src = AP(tensor=square_dram, offset=(t * TILE + r) * SQUARE,
                         ap=[[FIELDS, FIELDS], [2 * SQUARE, 2 * TPAIRS], [1, FIELDS]])
                sp.dma_start(tail_mat[lane, :, lane], src).then_inc(s_tail_mat, 16)
            sp.wait_ge(s_mlpact, 16)
            sp.dma_start(out.rearrange("b o -> o b"), y_sb).then_inc(s_out, 16)
            sp.wait_ge(s_out, 16)

        @block.gpsimd
        def _(pool):
            pool.memset(ident[:, :], 0.0).then_inc(s_ident, 1)
            pool.wait_ge(s_ident, 1)
            pool.affine_select(out=ident[:, :], in_=ident[:, :], compare_op=ALU.not_equal, fill=1.0,
                               base=0, pattern=[[-1, 128]], channel_multiplier=1).then_inc(s_ident, 1)

            def gather(t, f):
                return pool.indirect_dma_start(
                    out=rows[:, f, :], out_offset=None, in_=tables[f],
                    in_offset=bass.IndirectOffsetOnAxis(ap=ids_sb[:, t, f:f + 1], axis=0))

            pool.wait_ge(s_ids, 16)
            for f in range(FIELDS):
                gather(0, f).then_inc(s_field[f // XFIELDS], 16)
            for i, s in enumerate(s_field):
                pool.wait_ge(s, 16 * min(XFIELDS, FIELDS - XFIELDS * i))
            pool.dma_start(rows_dram[0], rows[:, :, :].rearrange("p f d -> p (f d)")).then_inc(s_rows_out, 16)
            for t in range(1, TILES):
                pool.wait_ge(s_rows_out, 16 * t)
                if t == 1:
                    pool.wait_ge(s_xpose, PRO)
                else:
                    pool.wait_ge(s_stage, 16 * (GROUPS + 1) * (t - 1))
                for f in range(FIELDS):
                    gather(t, f).then_inc(s_gather, 16)
                pool.wait_ge(s_gather, 16 * FIELDS * t)
                pool.dma_start(rows_dram[t], rows[:, :, :].rearrange("p f d -> p (f d)")).then_inc(s_rows_out, 16)
                if t >= 2:
                    pool.wait_ge(s_square, t - 1)
                    store_square(pool, t - 2, s_square_out)
            pool.wait_ge(s_square, TILES - 1)
            store_square(pool, TILES - 2, s_square_out)
            pool.wait_ge(s_z, 2 * GROUPS * (TILES - 1))
            pool.memset(tail_mat, 0.0).then_inc(s_tail_zero, 1)

        @block.vector
        def _(dve):
            nc.vector.memset(diag[0][:, :], 0.0).then_inc(s_zero, 1)
            nc.vector.memset(diag[1][:, :], 0.0).then_inc(s_zero, 1)
            nc.vector.memset(square[:, :], 0.0).then_inc(s_zero, 1)
            nc.vector.memset(ymat[:, :, :], 0.0).then_inc(s_zero, 1)
            dve.wait_ge(s_split_w, 2)
            nc.vector.tensor_tensor(w_lo[:, :], wT[:, :], w_hi[:, :], ALU.subtract).then_inc(s_split_w, 1)

            def products(dst, t, k, q, first, count):
                e, row = emb[t % 3], TILE * WIDE
                at = (2 * k + q) * WIDE
                a = AP(tensor=e, offset=at, ap=[[row, 128], [32 * WIDE, QUAD], [0, count], [1, FIELDS]])
                b = AP(tensor=e, offset=at + first, ap=[[row, 128], [32 * WIDE, QUAD], [1, count], [1, FIELDS]])
                o = dst.rearrange("p (g s i) -> p g s i", g=QUAD, i=FIELDS)
                return nc.vector.tensor_tensor(o, a, b, ALU.mult)

            def low_half(n, q):
                wait(dve, s_prod_s, n + 1)
                wait(dve, s_high, 2 * (n + 1))
                wait(dve, s_main, 3 * (n - 1))
                nc.vector.tensor_tensor(low[:, q, :], prod_s[:, q, :], high[:, q, :],
                                        ALU.subtract).then_inc(s_low, 1)

            def y_half(t, g, h):
                at = 2 * (GROUPS * t + g) + h
                dve.wait_ge(s_y, at + 1)
                wait(dve, s_z, at - 1)
                e = AP(tensor=emb[t % 3], offset=(16 * g + 8 * h) * WIDE,
                       ap=[[TILE * WIDE, 128], [WIDE, 8], [1, FIELDS]])
                nc.vector.tensor_tensor(ytmp[:, h, :].rearrange("p (b i) -> p b i", i=FIELDS), e,
                                        ps_y[:, h, 0:8 * FIELDS].rearrange("p (b i) -> p b i", i=FIELDS),
                                        ALU.mult).then_inc(s_ymul, 1)
                dve.wait_ge(s_ymul, at + 1)
                nc.vector.tensor_reduce(z_raw[:, bass.ds(TILE * t + 16 * g + 8 * h, 8)],
                                        ytmp[:, h, :].rearrange("p (b i) -> p b i", i=FIELDS),
                                        axis=AX, op=ALU.add).then_inc(s_z, 1)

            def softmax_max(t):
                dve.wait_ge(s_sc_out, t + 1)
                nc.vector.tensor_reduce(neg_max[:, :], scores[:, :], axis=AX, op=ALU.max,
                                        negate=True).then_inc(s_max, 1)

            def softmax_scale(t):
                dve.wait_ge(s_exp, t + 1)
                nc.vector.reciprocal(inv_total[:, :], total[:, :]).then_inc(s_inv, 1)
                dve.wait_ge(s_inv, t + 1)
                wait(dve, s_square_out, 32 * t)
                band = AP(tensor=square, offset=FIELDS,
                          ap=[[WIDE * FIELDS, 128], [FIELDS, SHIFTS], [FIELDS + 1, FIELDS]])
                nc.vector.tensor_scalar(band, expd[:, :].rearrange("p (s i) -> p s i", i=FIELDS),
                                        inv_total[:, 0:1], None, ALU.mult).then_inc(s_band, 1)
                dve.wait_ge(s_band, t + 1)
                nc.vector.tensor_tensor(folded[:, :], square[:, 0:SHIFTS * FIELDS],
                                        square[:, SQUARE:SQUARE + SHIFTS * FIELDS], ALU.add).then_inc(s_square, 1)

            def body(t, k, k0):
                if k0 == 0:
                    dve.wait_ge(s_emb, t + 1)
                    if t == 0:
                        dve.wait_ge(s_copied, PRO)
                if t > 0 and k0 == 2:
                    softmax_max(t - 1)
                if t > 0 and k0 == 3:
                    softmax_scale(t - 1)
                for q in range(2):
                    n = 2 * (BODIES * t + k) + q
                    if t == 0 and k0 == 0 and q == 0:
                        products(prod_d[:, q, :], t, k, q, 1, DIRECT).then_inc(s_prod_d, 1)
                    wait(dve, s_low, n - 1)
                    products(prod_s[:, q, :], t, k, q, DIRECT + 1, SPLIT).then_inc(s_prod_s, 1)
                    if t > 0 or k0 > 0 or q > 0:
                        low_half(n - 1, 1 - q)
                        wait(dve, s_main, 3 * (n - 2) + 1)
                        products(prod_d[:, q, :], t, k, q, 1, DIRECT).then_inc(s_prod_d, 1)
                    if t > 0 and FIRST_SIDE < k0 <= LAST_SIDE:
                        y_half(t - 1, k - FIRST_SIDE - 1, q)

            dve.wait_ge(s_zero, 4)
            run(dve, body)
            low_half(2 * BODIES * TILES - 1, 1)
            softmax_max(TILES - 1)
            softmax_scale(TILES - 1)
            for g in range(GROUPS):
                bank = (ps_y, ps_sc)[g % 2]
                dve.wait_ge(s_tail_y, g + 1)
                wait(dve, s_z, 2 * GROUPS * (TILES - 1))
                e = AP(tensor=emb[(TILES - 1) % 3], offset=16 * g * WIDE,
                       ap=[[TILE * WIDE, 128], [8 * WIDE, 2], [WIDE, 8], [1, FIELDS]])
                wait(dve, s_tail_z, g)
                nc.vector.tensor_tensor(ytmp[:, :, :].rearrange("p h (b i) -> p h b i", i=FIELDS), e,
                                        bank[:, :, 0:8 * FIELDS].rearrange("p h (b i) -> p h b i", i=FIELDS),
                                        ALU.mult).then_inc(s_tail_ymul, 1)
                dve.wait_ge(s_tail_ymul, g + 1)
                nc.vector.tensor_reduce(z_raw[:, EARLY + 16 * g:EARLY + 16 * (g + 1)],
                                        ytmp[:, :, :].rearrange("p h (b i) -> p (h b) i", i=FIELDS),
                                        axis=AX, op=ALU.add).then_inc(s_tail_z, 1)

        @block.scalar
        def _(act):
            def emb_copy(e, f, n, src):
                dst = AP(tensor=e, offset=f, ap=[[TILE * WIDE, 128], [1, n], [WIDE, TILE]])
                return nc.scalar.activation(dst, src, ACT.Copy)

            def emb_repeat(t, copied):
                act.wait_ge(s_copied, copied)
                v = emb[t % 3][:, :].rearrange("p (b f) -> p b f", f=WIDE)
                nc.scalar.activation(v[:, :, FIELDS:WIDE], v[:, :, 0:SHIFTS], ACT.Copy).then_inc(s_emb, 1)

            def make_diag(t, copied):
                act.wait_ge(s_copied, copied)
                if t >= 2:
                    for q in range(2):
                        act.wait_ge(s_pick[q], 16 * BODIES * (t - 1))
                dst = AP(tensor=diag[t % 2], offset=0, ap=[[QUADS * 128, 128], [129, QUADS], [32, QUAD]])
                src = AP(tensor=gT, offset=TILE * t, ap=[[BATCH, 128], [1, QUADS], [32, QUAD]])
                nc.scalar.activation(dst, src, ACT.Copy).then_inc(s_diag, 1)

            act.wait_ge(s_xpose, 1)
            nc.scalar.activation(wT[:, :], ps[:, 0, 0:128], ACT.Copy).then_inc(s_split_w, 1)
            nc.scalar.activation(gT[:, 0:TILE], ps[:, 0, 128:256], ACT.Copy).then_inc(s_copied, 1)
            act.wait_ge(s_split_w, 1)
            nc.scalar.activation(w_hi[:, :], wT[:, :], ACT.Copy).then_inc(s_split_w, 1)
            act.wait_ge(s_zero, 4)
            make_diag(0, 1)
            for v in range(1, PRO):
                f, n = XFIELDS * (v - 1), min(XFIELDS, FIELDS - XFIELDS * (v - 1))
                act.wait_ge(s_xpose, v + 1)
                emb_copy(emb[0], f, n, ps[:, 2 * (v % 2), 0:n * TILE].rearrange("p (f b) -> p f b", b=TILE))\
                    .then_inc(s_copied, 1)
                if f + n == SHIFTS:
                    emb_repeat(0, v + 1)
            act.wait_ge(s_wload, 48)

            def relu(n, q, j, slot):
                act.wait_ge(s_main, 3 * n + j + 1)
                if j == 0:
                    wait(act, s_scores, n - 1)
                if j == 0:
                    dst = AP(tensor=fm, offset=q * QUAD * PAIRS,
                             ap=[[2 * QUAD * PAIRS, 128], [2 * PAIRS, 2], [PAIRS, 2], [1, DCOLS]])
                    src = ps[:, 2 * slot:2 * slot + 2, 0:2 * DCOLS].rearrange("p c (g n) -> p c g n", g=2)
                else:
                    dst = AP(tensor=fm, offset=q * QUAD * PAIRS + 2 * (j - 1) * PAIRS + DCOLS,
                             ap=[[2 * QUAD * PAIRS, 128], [PAIRS, 2], [1, SCOLS]])
                    src = ps[:, 2 * slot:2 * slot + 2, 0:SCOLS]
                nc.scalar.activation(dst, src, ACT.Relu, bias=attn_b_sb[:, 0:1]).then_inc(s_relu, 1)

            def high_half(n, q, h):
                act.wait_ge(s_prod_s, n + 1)
                wait(act, s_main, 3 * (n - 2) + 2 + h)
                wait(act, s_low, n - 1)
                part = slice(2 * SCOLS * h, 2 * SCOLS * (h + 1))
                nc.scalar.activation(high[:, q, part], prod_s[:, q, part], ACT.Copy).then_inc(s_high, 1)

            def scores_out(t):
                act.wait_ge(s_scores, QUADS * (t + 1))
                wait(act, s_exp, t)
                nc.scalar.activation(scores[:, :].rearrange("p (c n) -> p c n", c=2), ps_sc[:, :, 0:HALF],
                                     ACT.Copy).then_inc(s_sc_out, 1)

            def exponentials(t):
                act.wait_ge(s_max, t + 1)
                wait(act, s_square_out, 32 * t)
                nc.scalar.activation(expd[:, :], scores[:, :], ACT.Exp, bias=neg_max[:, 0:1],
                                     accum_out=total[:, 0:1]).then_inc(s_exp, 1)

            def drain_start(t, k, q):
                n = 2 * (BODIES * t + k) + q
                relu(n, q, 0, (3 * q) % 2)
                relu(n, q, 1, (3 * q + 1) % 2)

            def drain_end(t, k, k0, q):
                n = 2 * (BODIES * t + k) + q
                slot = q % 2
                relu(n, q, 2, slot)
                if side_x(t, k0):
                    v = PRO + SIDE * t + 2 * (k - FIRST_SIDE) + q
                    act.wait_ge(s_xpose, v + 1)
                    if k0 < LAST_SIDE:
                        emb_copy(emb[(t + 1) % 3], XFIELDS * (k - FIRST_SIDE) + 2 * q, 2,
                                 ps[:, 2 * slot:2 * slot + 2, SCOLS:SCOLS + TILE]).then_inc(s_copied, 1)
                    elif q == 0:
                        emb_copy(emb[(t + 1) % 3], FIELDS - 1, 1,
                                 ps[:, 2 * slot:2 * slot + 1, SCOLS:SCOLS + TILE]).then_inc(s_copied, 1)
                        emb_repeat(t + 1, v + 1)
                    else:
                        nc.scalar.activation(gT[:, TILE * (t + 1):TILE * (t + 2)],
                                             ps[:, 2 * slot, SCOLS:SCOLS + TILE], ACT.Copy).then_inc(s_copied, 1)
                        make_diag(t + 1, v + 1)

            def body(t, k, k0, dt, dk, dk0):
                for q in range(2):
                    if dt >= 0:
                        drain_start(dt, dk, q)
                    if q == 0 and t > 0 and k0 == 1:
                        scores_out(t - 1)
                    high_half(2 * (BODIES * t + k) + q, q, 0)
                    if dt >= 0:
                        drain_end(dt, dk, dk0, q)
                    high_half(2 * (BODIES * t + k) + q, q, 1)
                if t > 0 and k0 == 2:
                    exponentials(t - 1)

            for t, k, n in segments():
                if n == 1:
                    body(t, k, k, t if k else t - 1, (k - 1) % BODIES, (k - 1) % BODIES)
                else:
                    with act.Fori(0, n) as i:
                        body(t, k + i, k, t, k - 1 + i, k - 1)
            for q in range(2):
                drain_start(TILES - 1, BODIES - 1, q)
                drain_end(TILES - 1, BODIES - 1, BODIES - 1, q)
            scores_out(TILES - 1)
            act.wait_ge(s_mlpload, 80)
            act.wait_ge(s_z, 2 * GROUPS * (TILES - 1))
            nc.scalar.activation(zT[:, 0:EARLY], z_raw[:, 0:EARLY], ACT.Copy, scale=100.0).then_inc(s_mlpact, 1)
            exponentials(TILES - 1)

            def hidden1(c0, n, done, bank):
                for m in range(4):
                    act.wait_ge(s_mlp, done + m + 1)
                    nc.scalar.activation(h1[:, m * BATCH + c0:m * BATCH + c0 + n], bank(m), ACT.Relu,
                                         bias=b1_sb[:, m:m + 1]).then_inc(s_mlpact, 1)

            def hidden2(c0, n, done, bank):
                for m in range(2):
                    act.wait_ge(s_mlp, done + m + 1)
                    nc.scalar.activation(h2[:, m * BATCH + c0:m * BATCH + c0 + n], bank(m), ACT.Relu,
                                         bias=b2_sb[:, m:m + 1]).then_inc(s_mlpact, 1)

            hidden1(0, EARLY, 0, lambda m: ps[:, m, 0:EARLY])
            hidden2(0, EARLY, 4, lambda m: ps[:, m, 0:EARLY])
            act.wait_ge(s_mlp, 7)
            act.wait_ge(s_tail_z, GROUPS)
            nc.scalar.activation(zT[:, EARLY:BATCH], z_raw[:, EARLY:BATCH], ACT.Copy, scale=100.0).then_inc(s_mlpact, 1)
            nc.scalar.activation(y_sb[:, 0:EARLY], ps[0:1, 2, 0:EARLY], ACT.Copy).then_inc(s_mlpact, 1)
            act.wait_ge(s_mlp, 11)
            hidden1(EARLY, TILE, 7, lambda m: ps[:, 3, m * TILE:(m + 1) * TILE])
            act.wait_ge(s_mlp, 13)
            hidden2(EARLY, TILE, 11, lambda m: ps[:, 0, m * TILE:(m + 1) * TILE])
            act.wait_ge(s_mlp, 14)
            nc.scalar.activation(y_sb[:, EARLY:BATCH], ps[0:1, 1, 0:TILE], ACT.Copy).then_inc(s_mlpact, 1)

        @block.tensor
        def _(pe):
            pe.wait_ge(s_ident, 2)
            pe.wait_ge(s_wload, 48)
            nc.tensor.transpose(ps[:, 0, 0:128], wn[:, :], ident[:, :])
            nc.tensor.transpose(ps[:, 0, 128:256], gnn_sb[:, 0, :], ident[:, :]).then_inc(s_xpose, 1)
            for v in range(1, PRO):
                f, n = XFIELDS * (v - 1), min(XFIELDS, FIELDS - XFIELDS * (v - 1))
                pe.wait_ge(s_field[v - 1], 16 * n)
                if v >= 2:
                    pe.wait_ge(s_copied, v - 1)
                for c in range(n):
                    last = nc.tensor.transpose(ps[:, 2 * (v % 2), c * TILE:(c + 1) * TILE],
                                               rows[:, f + c, :], ident[:, :])
                last.then_inc(s_xpose, 1)
            pe.wait_ge(s_split_w, 3)

            def multiply(t, k, k0, q, steps):
                n = 2 * (BODIES * t + k) + q
                for j in steps:
                    m = 3 * n + j
                    slot = (3 * q + j) % 2
                    if j == 0:
                        pe.wait_ge(s_prod_d, n + 1)
                    if j == 1:
                        pe.wait_ge(s_low, n + 1)
                    if j < 2 and t == 0 and k0 == 0 and q == 0:
                        pe.wait_ge(s_copied, PRO)
                    elif j < 2 or not side_x(t, k0):
                        wait(pe, s_relu, m - 1)
                    if j == 1 and t < TILES - 1 and FIRST_SIDE <= k0 <= LAST_SIDE + 1 and (q == 0 or k0 <= LAST_SIDE):
                        pe.wait_ge(s_copied, PRO + SIDE * t + 2 * (k - FIRST_SIDE) + q)
                    if j == 0:
                        for c in range(2):
                            last = nc.tensor.matmul(ps[:, 2 * slot + c, 0:2 * DCOLS], wT[:, :],
                                                    prod_d[:, q, c * 2 * DCOLS:(c + 1) * 2 * DCOLS],
                                                    start=True, stop=True)
                    else:
                        for a, (w, p) in enumerate(((w_hi, high), (w_hi, low), (w_lo, high))):
                            for c in range(2):
                                g = 2 * (j - 1) + c
                                last = nc.tensor.matmul(ps[:, 2 * slot + c, 0:SCOLS], w[:, :],
                                                        p[:, q, g * SCOLS:(g + 1) * SCOLS],
                                                        start=(a == 0), stop=(a == 2))
                    last.then_inc(s_main, 1)

            def transposes(t, k, k0, q):
                slot = q % 2
                pe.wait_ge(s_relu, 3 * (2 * (BODIES * t + k) + q) + 1)
                if q == 0:
                    pe.wait_ge(s_stage, 16 * ((GROUPS + 1) * t + k - FIRST_SIDE + 1))
                if k0 < LAST_SIDE:
                    for c in range(2):
                        last = nc.tensor.transpose(ps[:, 2 * slot + c, SCOLS:SCOLS + TILE],
                                                   stage[:, (2 * q + c) * DIM:(2 * q + c + 1) * DIM], ident[:, :])
                elif q == 0:
                    last = nc.tensor.transpose(ps[:, 2 * slot, SCOLS:SCOLS + TILE], stage[:, 0:DIM], ident[:, :])
                else:
                    last = nc.tensor.transpose(ps[:, 2 * slot, SCOLS:SCOLS + TILE], gnn_sb[:, t + 1, :], ident[:, :])
                last.then_inc(s_xpose, 1)

            def score(n, q, first, last_quad):
                pe.wait_ge(s_relu, 3 * n + 3)
                for c in range(2):
                    for g in range(QUAD):
                        last = nc.tensor.matmul(ps_sc[32 * g:32 * g + 32, c, 0:HALF],
                                                pick[:, q, 32 * g:32 * g + 32],
                                                fm[:, q, g * PAIRS + c * HALF:g * PAIRS + (c + 1) * HALF],
                                                start=first, stop=last_quad)
                last.then_inc(s_scores, 1)

            def y_multiply(t, g, h):
                at = 2 * (GROUPS * t + g) + h
                if h == 0:
                    pe.wait_ge(s_ylo, 64 * (GROUPS * t + g + 1))
                wait(pe, s_ymul, at - 1)
                for m in range(YPAIRS // 2):
                    last = nc.tensor.matmul(ps_y[:, h, m * YCOLS:(m + 1) * YCOLS], yrows[:, YPAIRS // 2 * h + m, :],
                                            ymat[:, YPAIRS // 2 * h + m, :], start=True, stop=True)
                last.then_inc(s_y, 1)

            def body(t, k, k0):
                for q in range(2):
                    n = 2 * (BODIES * t + k) + q
                    multiply(t, k, k0, q, (0, 1))
                    if t > 0 or k0 > 0 or q > 0:
                        pe.wait_ge(s_pick[1 - q], 16 * (BODIES * t + k + q))
                        first = k0 == 0 and q == 1
                        if first and t > 0:
                            pe.wait_ge(s_sc_out, t)
                        score(n - 1, 1 - q, first, k0 == 0 and q == 0)
                    if side_x(t, k0):
                        transposes(t, k, k0, q)
                    multiply(t, k, k0, q, (2,))
                    if side_y(t, k0):
                        y_multiply(t - 1, k - FIRST_SIDE, q)

            run(pe, body)
            pe.wait_ge(s_pick[1], 16 * BODIES * TILES)
            score(2 * BODIES * TILES - 1, 1, False, True)

            def layer1(c0, n, bank):
                for m in range(4):
                    for c, rhs in enumerate((gT, zT, gT)):
                        last = nc.tensor.matmul(bank(m), w1_sb[:, c, m * 128:(m + 1) * 128], rhs[:, c0:c0 + n],
                                                start=(c == 0), stop=(c == 2))
                    last.then_inc(s_mlp, 1)

            def layer2(m, c0, n, bank):
                for c in range(4):
                    last = nc.tensor.matmul(bank(m), w2_sb[:, c, m * 128:(m + 1) * 128],
                                            h1[:, c * BATCH + c0:c * BATCH + c0 + n], start=(c == 0), stop=(c == 3))
                last.then_inc(s_mlp, 1)

            def layer3(c0, n, bank):
                for c in range(2):
                    last = nc.tensor.matmul(bank, w3_sb[:, c:c + 1], h2[:, c * BATCH + c0:c * BATCH + c0 + n],
                                            start=(c == 0), stop=(c == 1))
                last.then_inc(s_mlp, 1)

            pe.wait_ge(s_mlpload, 80)
            pe.wait_ge(s_mlpact, 1)
            pe.wait_ge(s_relu, 3 * QUADS * TILES)
            layer1(0, EARLY, lambda m: ps[:, m, 0:EARLY])
            pe.wait_ge(s_tail_rows, 64)
            pe.wait_ge(s_tail_mat, 32)
            pe.wait_ge(s_sc_out, TILES)
            for g in range(GROUPS):
                bank = (ps_y, ps_sc)[g % 2]
                wait(pe, s_tail_ymul, g - 1)
                for m in range(YPAIRS):
                    at = YPAIRS * g + m
                    c, h = m % (YPAIRS // 2), m // (YPAIRS // 2)
                    last = nc.tensor.matmul(bank[:, h, c * YCOLS:(c + 1) * YCOLS],
                                            tail_rows[at // TPAIRS][:, at % TPAIRS, :], tail_mat[:, at, :],
                                            start=True, stop=True)
                last.then_inc(s_tail_y, 1)
                if g in (2, 4):
                    pe.wait_ge(s_mlpact, 5)
                    layer2((g - 2) // 2, 0, EARLY, lambda m: ps[:, m, 0:EARLY])
            pe.wait_ge(s_mlpact, 7)
            layer3(0, EARLY, ps[0:1, 2, 0:EARLY])
            pe.wait_ge(s_mlpact, 8)
            layer1(EARLY, TILE, lambda m: ps[:, 3, m * TILE:(m + 1) * TILE])
            pe.wait_ge(s_mlpact, 13)
            for m in range(2):
                layer2(m, EARLY, TILE, lambda m: ps[:, 0, m * TILE:(m + 1) * TILE])
            pe.wait_ge(s_mlpact, 15)
            layer3(EARLY, TILE, ps[0:1, 1, 0:TILE])


def kernel(**inputs):
    import numpy as _np
    import concourse.bacc as _bacc
    from concourse import mybir as _mybir
    from concourse.bass_utils import run_bass_kernel_spmd as _run

    nc = _bacc.Bacc("TRN2", target_bir_lowering=False, num_devices=1)
    arrays, aps = {}, {}
    for name, value in inputs.items():
        a = _np.ascontiguousarray(value)
        arrays[f"in_{name}_dram"] = a
        aps[name] = nc.dram_tensor(f"in_{name}_dram", a.shape, _mybir.dt.from_np(a.dtype), kind="ExternalInput").ap()
    out = nc.dram_tensor("out_0_dram", (BATCH, 1), _mybir.dt.float32, kind="ExternalOutput").ap()
    field_attention_tower(nc, aps["r_gnn_feature"], aps["ids"], [aps[f"tbl_{f}"] for f in range(FIELDS)],
                          aps["W_top1"], aps["b_top1"], aps["W_top2"], aps["b_top2"], aps["W_top3"],
                          aps["L0_rec_attn_W"], aps["L0_rec_attn_b"], out)
    r = _run(nc, [arrays], core_ids=[0])
    return r.results[0]["out_0_dram"]
```

```python
from contextlib import ExitStack

import numpy as np

import concourse.bass as bass
from concourse import mybir

BATCH = 512
FIELDS = 33
DIM = 128
TILE = 128
TILES = BATCH // TILE
SHIFTS = FIELDS // 2
PAIRS = SHIFTS * FIELDS
WIDE = FIELDS + SHIFTS
QUAD = 4
QUADS = TILE // QUAD
BODIES = QUADS // 2
DIRECT = 6
SPLIT = SHIFTS - DIRECT
DCOLS = DIRECT * FIELDS
SCOLS = SPLIT * FIELDS
HALF = PAIRS // 2
BANK = 512
STACK = 3
YTRIPLES = 3
YROWS = STACK * YTRIPLES
YCOLS = STACK * FIELDS
YSHARES = -(-TILE // YROWS)
YREST = TILE - (YSHARES - 1) * YROWS
GROUPS = (YSHARES + 1) // 2
YLOADS = ((GROUPS - 1) * (1 + STACK) + 1 + YREST, (GROUPS - 1) * (1 + STACK))
TSTACKS = -(-TILE // STACK)
TGROUP = 8
EARLY = BATCH - TILE
SQUARE = FIELDS * FIELDS
FIRST_SIDE = 5
LAST_SIDE = FIRST_SIDE + GROUPS
REPEATS = 4
XFIELDS = 4
PRO = 10
SIDE = 2 * GROUPS + 2
HID1 = 512
HID2 = 256


def field_attention_tower(nc, gnn, ids, tables, w1, b1, w2, b2, w3, attn_w, attn_b, out):
    f32 = mybir.dt.float32
    f32r = mybir.dt.float32r
    ALU = mybir.AluOpType
    ACT = mybir.ActivationFunctionType
    AX = mybir.AxisListType.X
    AP = bass.AP

    rows_dram = nc.dram_tensor("rows_scratch", (TILES, TILE, FIELDS * DIM), f32)
    square_dram = nc.dram_tensor("square_scratch", (TILES, TILE, SQUARE), f32)

    with ExitStack() as ctx:
        def sb(name, shape, dt=f32):
            return ctx.enter_context(nc.sbuf_tensor(name, shape, dt))

        def sem(name):
            return ctx.enter_context(nc.semaphore(name))

        ids_sb = sb("ids_sb", [128, TILES, FIELDS], mybir.dt.int32)
        rows = sb("rows", [128, FIELDS, DIM])
        stage = sb("stage", [128, XFIELDS * DIM])
        emb = [sb(f"emb{i}", [128, TILE * WIDE]) for i in range(3)]
        prod_d = sb("prod_d", [128, 2, QUAD * DCOLS])
        prod_s = sb("prod_s", [128, 2, QUAD * SCOLS])
        high = sb("high", [128, 2, QUAD * SCOLS], f32r)
        low = sb("low", [128, 2, QUAD * SCOLS], f32r)
        fm = sb("fm", [128, 2, QUAD * PAIRS])
        gnn_sb = sb("gnn_sb", [128, TILES, DIM])
        gT = sb("gT", [128, BATCH])
        diag = [sb(f"diag{i}", [128, QUADS * QUAD * 32]) for i in range(2)]
        pick = sb("pick", [128, 2, QUAD * 32])
        wn = sb("wn", [128, DIM])
        wT = sb("wT", [128, 128])
        w_hi = sb("w_hi", [128, 128], f32r)
        w_lo = sb("w_lo", [128, 128], f32r)
        ident = sb("ident", [128, 128])
        attn_b_sb = sb("attn_b_sb", [128, 1])
        scores = sb("scores", [128, PAIRS])
        expd = sb("expd", [128, PAIRS])
        neg_max = sb("neg_max", [128, 1])
        total = sb("total", [128, 1])
        inv_total = sb("inv_total", [128, 1])
        square = sb("square", [128, WIDE * FIELDS])
        folded = expd
        yrows = sb("yrows", [YCOLS, 2 * YTRIPLES, DIM])
        ymat = sb("ymat", [YCOLS, 2 * YTRIPLES, YCOLS])
        ytmp = sb("ytmp", [128, 2, YROWS * FIELDS])
        zT = sb("zT", [128, BATCH])
        w3_sb = sb("w3_sb", [128, 2])
        b1_sb = sb("b1_sb", [128, 4])
        b2_sb = sb("b2_sb", [128, 2])
        tail_rows = emb[1][0:YCOLS, 0:TSTACKS * DIM].rearrange("p (m d) -> p m d", d=DIM)
        tail_mat = emb[2][0:YCOLS, 0:TSTACKS * YCOLS].rearrange("p (m i) -> p m i", i=YCOLS)
        tail_tmp = prod_s[:, :, 0:TGROUP * YCOLS]
        w1_sb = diag[0][:, 0:3 * HID1].rearrange("p (c n) -> p c n", c=3)
        w2_sb = diag[0][:, 3 * HID1:3 * HID1 + 4 * HID2].rearrange("p (c n) -> p c n", c=4)
        h1 = fm[:, :, :].rearrange("p a n -> p (a n)")[:, 0:4 * BATCH]
        h2 = fm[:, :, :].rearrange("p a n -> p (a n)")[:, 4 * BATCH:6 * BATCH]
        y_sb = ytmp[0:1, :, :].rearrange("p h n -> p (h n)")[:, 0:BATCH]

        ps = ctx.enter_context(nc.psum_tensor("ps", [128, 4, BANK], f32))
        ps_sc = ctx.enter_context(nc.psum_tensor("ps_sc", [128, 2, BANK], f32))
        ps_y = ctx.enter_context(nc.psum_tensor("ps_y", [128, 2, BANK], f32))

        s_ids = sem("s_ids")
        s_wload = sem("s_wload")
        s_mlpload = sem("s_mlpload")
        s_ident = sem("s_ident")
        s_zero = sem("s_zero")
        s_field = [sem(f"s_field{i}") for i in range(9)]
        s_gather = [sem("s_gather_low"), sem("s_gather_high")]
        s_rows_out = sem("s_rows_out")
        s_stage = sem("s_stage")
        s_emb = sem("s_emb")
        s_diag = sem("s_diag")
        s_pick = [sem("s_pick0"), sem("s_pick1")]
        s_split_w = sem("s_split_w")
        s_prod_d = sem("s_prod_d")
        s_prod_s = sem("s_prod_s")
        s_high = sem("s_high")
        s_low = sem("s_low")
        s_main = sem("s_main")
        s_relu = sem("s_relu")
        s_xpose = sem("s_xpose")
        s_copied = sem("s_copied")
        s_scores = sem("s_scores")
        s_sc_out = sem("s_sc_out")
        s_max = sem("s_max")
        s_exp = sem("s_exp")
        s_inv = sem("s_inv")
        s_band = sem("s_band")
        s_square = sem("s_square")
        s_square_out = sem("s_square_out")
        s_square_last = sem("s_square_last")
        s_yload = [sem(f"s_yload{h}") for h in range(2)]
        s_y = sem("s_y")
        s_ymul = sem("s_ymul")
        s_z = sem("s_z")
        s_tail_rows = sem("s_tail_rows")
        s_tail_zero = sem("s_tail_zero")
        s_tail_mat = sem("s_tail_mat")
        s_tail_y = sem("s_tail_y")
        s_tail_ymul = sem("s_tail_ymul")
        s_tail_z = sem("s_tail_z")
        s_w1 = sem("s_w1")
        s_mlp = sem("s_mlp")
        s_mlpact = sem("s_mlpact")
        s_out = sem("s_out")

        def segments():
            for t in range(TILES):
                for k in range(FIRST_SIDE + 2):
                    yield t, k, 1
                yield t, FIRST_SIDE + 2, GROUPS - 3
                for k in range(LAST_SIDE - 1, BODIES):
                    yield t, k, 1

        def run(eng, body):
            for t, k, n in segments():
                if n == 1:
                    body(t, k, k)
                else:
                    with eng.Fori(0, n) as i:
                        body(t, k + i, k)

        def wait(eng, s, v):
            if not isinstance(v, int) or v > 0:
                eng.wait_ge(s, v)

        def side_x(t, k0):
            return t < TILES - 1 and FIRST_SIDE <= k0 <= LAST_SIDE

        def side_y(t, k0):
            return t > 0 and FIRST_SIDE <= k0 < LAST_SIDE

        def store_square(eng, t, stored):
            dst = square_dram[t]
            eng.dma_start(dst[:, 0:SHIFTS * FIELDS], folded[:, :]).then_inc(stored, 16)
            eng.dma_start(dst[:, SHIFTS * FIELDS:SQUARE], square[:, SHIFTS * FIELDS:SQUARE]).then_inc(stored, 16)

        block = ctx.enter_context(nc.Block())

        @block.sync
        def _(sp):
            sp.dma_start(ids_sb[:, :, :], ids.rearrange("(t p) f -> p t f", p=128)).then_inc(s_ids, 16)
            sp.dma_start(wn[:, :], attn_w).then_inc(s_wload, 16)
            sp.dma_start(gnn_sb[:, :, :], gnn.rearrange("(t p) a -> p t a", p=128)).then_inc(s_wload, 16)
            sp.dma_start(attn_b_sb[:, :], attn_b.rearrange("(a o) -> a o", o=1)).then_inc(s_wload, 16)
            with nc.allow_non_contiguous_dma(reason="a few hundred words of biases and output weights"):
                sp.dma_start(w3_sb[:, :], w3.rearrange("(c p) o -> p (c o)", p=128)).then_inc(s_mlpload, 16)
                sp.dma_start(b1_sb[:, :], b1.rearrange("(c p) -> p c", p=128)).then_inc(s_mlpload, 16)
                sp.dma_start(b2_sb[:, :], b2.rearrange("(c p) -> p c", p=128)).then_inc(s_mlpload, 16)

            def pick_load(t, k, q):
                sp.wait_ge(s_diag, t + 1)
                wait(sp, s_scores, 2 * (BODIES * t + k) + q - 1)
                sp.dma_start(pick[:, q, :], diag[t % 2][:, bass.ds((2 * k + q) * 128, 128)]).then_inc(s_pick[q], 16)

            def side_loads(t, g, h):
                first_group = isinstance(g, int) and g == 0
                last_group = isinstance(g, int) and g == GROUPS - 1
                wait(sp, s_y, YSHARES * t if first_group else YSHARES * t + 2 * g + h - 1)
                stacked, n = (YREST, 1) if last_group else (STACK, YTRIPLES)
                row = t * TILE + 2 * YROWS * g + YROWS * h
                src = AP(tensor=rows_dram, offset=row * (FIELDS * DIM),
                         ap=[[DIM, stacked * FIELDS], [STACK * FIELDS * DIM, n], [1, DIM]])
                sp.dma_start(yrows[0:stacked * FIELDS, YTRIPLES * h:YTRIPLES * h + n, :], src)\
                    .then_inc(s_yload[h], 16)
                for r in range(stacked):
                    lane = slice(FIELDS * r, FIELDS * (r + 1))
                    src = AP(tensor=square_dram, offset=(row + r) * SQUARE,
                             ap=[[FIELDS, FIELDS], [STACK * SQUARE, n], [1, FIELDS]])
                    sp.dma_start(ymat[lane, YTRIPLES * h:YTRIPLES * h + n, lane], src).then_inc(s_yload[h], 16)

            def body(t, k, k0):
                pick_load(t, k, 0)
                if FIRST_SIDE - 1 <= k0 < LAST_SIDE - 1 and t > 0:
                    if k0 == FIRST_SIDE - 1:
                        sp.wait_ge(s_rows_out, 16 * t)
                        sp.wait_ge(s_square_out, 32 * t)
                    side_loads(t - 1, k - FIRST_SIDE + 1, 0)
                pick_load(t, k, 1)
                if FIRST_SIDE - 1 <= k0 < LAST_SIDE - 2 and t > 0:
                    side_loads(t - 1, k - FIRST_SIDE + 1, 1)
                if FIRST_SIDE - 1 <= k0 < LAST_SIDE and t < TILES - 1:
                    if k0 == FIRST_SIDE - 1:
                        sp.wait_ge(s_gather[0], 16 * SHIFTS * (t + 1))
                    else:
                        sp.wait_ge(s_gather[1], 16 * (FIELDS - SHIFTS) * (t + 1))
                    sp.wait_ge(s_xpose, PRO + SIDE * t + 2 * (k - FIRST_SIDE + 1))
                    if k0 == LAST_SIDE - 1:
                        sp.dma_start(stage[:, 0:DIM], rows[:, FIELDS - 1, :]).then_inc(s_stage, 16)
                    else:
                        sp.dma_start(stage[:, :], rows[:, bass.ds(XFIELDS * (k - FIRST_SIDE + 1), XFIELDS), :]
                                     .rearrange("p f d -> p (f d)")).then_inc(s_stage, 16)

            def last_tile_loads(k):
                if k < STACK:
                    sp.wait_ge(s_rows_out, 16 * TILES)
                    sp.wait_ge(s_z, YSHARES * (TILES - 2))
                    n = -(-(TILE - k) // STACK)
                    src = AP(tensor=rows_dram, offset=((TILES - 1) * TILE + k) * FIELDS * DIM,
                             ap=[[DIM, FIELDS], [STACK * FIELDS * DIM, n], [1, DIM]])
                    sp.dma_start(tail_rows[FIELDS * k:FIELDS * (k + 1), 0:n, :], src).then_inc(s_tail_rows, 16)
                elif k == STACK:
                    for q in range(2):
                        sp.wait_ge(s_pick[q], 16 * BODIES * (TILES - 1))
                    sp.dma_start(w1_sb, w1.rearrange("(c p) n -> p c n", p=128)).then_inc(s_mlpload, 16)
                else:
                    sp.dma_start(w2_sb, w2.rearrange("(c p) n -> p c n", p=128)).then_inc(s_mlpload, 16)

            for t in range(TILES):
                for k in range(FIRST_SIDE):
                    body(t, k, k)
                    if t == TILES - 1:
                        last_tile_loads(k)
                with sp.Fori(FIRST_SIDE, LAST_SIDE - 2) as k:
                    body(t, k, FIRST_SIDE)
                for k in range(LAST_SIDE - 2, BODIES):
                    body(t, k, k)
            t = TILES - 1
            sp.wait_ge(s_square, TILES)
            store_square(sp, t, s_square_last)
            sp.wait_ge(s_square_last, 32)
            sp.wait_ge(s_tail_zero, 1)
            for r in range(STACK):
                n = -(-(TILE - r) // STACK)
                lane = slice(FIELDS * r, FIELDS * (r + 1))
                src = AP(tensor=square_dram, offset=(t * TILE + r) * SQUARE,
                         ap=[[FIELDS, FIELDS], [STACK * SQUARE, n], [1, FIELDS]])
                sp.dma_start(tail_mat[lane, 0:n, lane], src).then_inc(s_tail_mat, 16)
            sp.wait_ge(s_mlpact, 14)
            sp.dma_start(out.rearrange("b o -> o b"), y_sb).then_inc(s_out, 16)
            sp.wait_ge(s_out, 16)

        @block.gpsimd
        def _(pool):
            pool.memset(ident[:, :], 0.0).then_inc(s_ident, 1)
            pool.wait_ge(s_ident, 1)
            pool.affine_select(out=ident[:, :], in_=ident[:, :], compare_op=ALU.not_equal, fill=1.0,
                               base=0, pattern=[[-1, 128]], channel_multiplier=1).then_inc(s_ident, 1)

            def gather(t, f):
                return pool.indirect_dma_start(
                    out=rows[:, f, :], out_offset=None, in_=tables[f],
                    in_offset=bass.IndirectOffsetOnAxis(ap=ids_sb[:, t, f:f + 1], axis=0))

            pool.wait_ge(s_ids, 16)
            for f in range(FIELDS):
                gather(0, f).then_inc(s_field[f // XFIELDS], 16)
            for i, s in enumerate(s_field):
                pool.wait_ge(s, 16 * min(XFIELDS, FIELDS - XFIELDS * i))
            pool.dma_start(rows_dram[0], rows[:, :, :].rearrange("p f d -> p (f d)")).then_inc(s_rows_out, 16)
            for t in range(1, TILES):
                pool.wait_ge(s_rows_out, 16 * t)
                if t == 1:
                    pool.wait_ge(s_xpose, PRO)
                else:
                    pool.wait_ge(s_stage, 16 * (GROUPS + 1) * (t - 1))
                for f in range(FIELDS):
                    gather(t, f).then_inc(s_gather[f // SHIFTS > 0], 16)
                pool.wait_ge(s_gather[0], 16 * SHIFTS * t)
                pool.wait_ge(s_gather[1], 16 * (FIELDS - SHIFTS) * t)
                pool.dma_start(rows_dram[t], rows[:, :, :].rearrange("p f d -> p (f d)")).then_inc(s_rows_out, 16)
                if t >= 2:
                    pool.wait_ge(s_square, t - 1)
                    store_square(pool, t - 2, s_square_out)
            pool.wait_ge(s_square, TILES - 1)
            store_square(pool, TILES - 2, s_square_out)
            pool.wait_ge(s_z, YSHARES * (TILES - 1))
            pool.memset(tail_mat, 0.0).then_inc(s_tail_zero, 1)

        @block.vector
        def _(dve):
            nc.vector.memset(diag[0][:, :], 0.0).then_inc(s_zero, 1)
            nc.vector.memset(diag[1][:, :], 0.0).then_inc(s_zero, 1)
            nc.vector.memset(square[:, :], 0.0).then_inc(s_zero, 1)
            nc.vector.memset(ymat[:, :, :], 0.0).then_inc(s_zero, 1)
            dve.wait_ge(s_split_w, 2)
            nc.vector.tensor_tensor(w_lo[:, :], wT[:, :], w_hi[:, :], ALU.subtract).then_inc(s_split_w, 1)

            def products(dst, t, k, q, first, count, i0=0, n=FIELDS):
                e, row = emb[t % 3], TILE * WIDE
                at = (2 * k + q) * WIDE + i0
                a = AP(tensor=e, offset=at, ap=[[row, 128], [32 * WIDE, QUAD], [0, count], [1, n]])
                b = AP(tensor=e, offset=at + first, ap=[[row, 128], [32 * WIDE, QUAD], [1, count], [1, n]])
                o = dst.rearrange("p (g s i) -> p g s i", g=QUAD, i=FIELDS)[:, :, :, i0:i0 + n]
                return nc.vector.tensor_tensor(o, a, b, ALU.mult)

            def low_half(n, q):
                wait(dve, s_prod_s, n + 1)
                wait(dve, s_high, 2 * (n + 1))
                wait(dve, s_main, 3 * (n - 1))
                nc.vector.tensor_tensor(low[:, q, :], prod_s[:, q, :], high[:, q, :],
                                        ALU.subtract).then_inc(s_low, 1)

            def y_part(t, g, h):
                last = isinstance(g, int) and g == GROUPS - 1
                return 2 * YROWS * g + YROWS * h, YREST if last else YROWS, YSHARES * t + 2 * g + h

            def y_products(t, g, h):
                row, n, at = y_part(t, g, h)
                dve.wait_ge(s_y, at + 1)
                wait(dve, s_z, at if isinstance(g, int) and g + h == 0 else at - 1)
                e = AP(tensor=emb[t % 3], offset=row * WIDE, ap=[[TILE * WIDE, 128], [WIDE, n], [1, FIELDS]])
                nc.vector.tensor_tensor(ytmp[:, h, 0:n * FIELDS].rearrange("p (b i) -> p b i", i=FIELDS), e,
                                        ps_y[:, h, 0:n * FIELDS].rearrange("p (b i) -> p b i", i=FIELDS),
                                        ALU.mult).then_inc(s_ymul, 1)

            def y_sum(t, g, h):
                row, n, at = y_part(t, g, h)
                dve.wait_ge(s_ymul, at + 1)
                nc.vector.tensor_reduce(zT[:, bass.ds(TILE * t + row, n)],
                                        ytmp[:, h, 0:n * FIELDS].rearrange("p (b i) -> p b i", i=FIELDS),
                                        axis=AX, op=ALU.add).then_inc(s_z, 1)

            def softmax_max(t):
                dve.wait_ge(s_sc_out, t + 1)
                nc.vector.tensor_reduce(neg_max[:, :], scores[:, :], axis=AX, op=ALU.max,
                                        negate=True).then_inc(s_max, 1)

            def softmax_scale(t):
                dve.wait_ge(s_exp, t + 1)
                nc.vector.reciprocal(inv_total[:, :], total[:, :]).then_inc(s_inv, 1)
                dve.wait_ge(s_inv, t + 1)
                wait(dve, s_square_out, 32 * t)
                band = AP(tensor=square, offset=FIELDS,
                          ap=[[WIDE * FIELDS, 128], [FIELDS, SHIFTS], [FIELDS + 1, FIELDS]])
                nc.vector.tensor_scalar(band, expd[:, :].rearrange("p (s i) -> p s i", i=FIELDS),
                                        inv_total[:, 0:1], 100.0, ALU.mult, ALU.mult).then_inc(s_band, 1)
                dve.wait_ge(s_band, t + 1)
                nc.vector.tensor_tensor(folded[:, :], square[:, 0:SHIFTS * FIELDS],
                                        square[:, SQUARE:SQUARE + SHIFTS * FIELDS], ALU.add).then_inc(s_square, 1)

            def body(t, k, k0):
                i0 = 0
                if k0 == 0:
                    dve.wait_ge(s_emb, REPEATS * (t + 1))
                    if t == 0:
                        i0 = XFIELDS * (PRO - 3) - SHIFTS
                        dve.wait_ge(s_copied, PRO - 2)
                        for q in range(2):
                            products(prod_d[:, q, :], 0, 0, q, 1, DIRECT, 0, i0)
                            products(prod_s[:, q, :], 0, 0, q, DIRECT + 1, SPLIT, 0, i0)
                        dve.wait_ge(s_copied, PRO)
                if t > 0 and k0 == 2:
                    softmax_max(t - 1)
                if t > 0 and k0 == 3:
                    softmax_scale(t - 1)
                for q in range(2):
                    n = 2 * (BODIES * t + k) + q
                    if t == 0 and k0 == 0 and q == 0:
                        products(prod_d[:, q, :], t, k, q, 1, DIRECT, i0, FIELDS - i0).then_inc(s_prod_d, 1)
                    wait(dve, s_low, n - 1)
                    products(prod_s[:, q, :], t, k, q, DIRECT + 1, SPLIT, i0, FIELDS - i0).then_inc(s_prod_s, 1)
                    if t > 0 and q == 0 and FIRST_SIDE + 1 < k0 <= LAST_SIDE:
                        y_sum(t - 1, k - FIRST_SIDE - 2, 1)
                    if t > 0 and q == 1 and FIRST_SIDE < k0 <= LAST_SIDE:
                        y_sum(t - 1, k - FIRST_SIDE - 1, 0)
                    if t > 0 or k0 > 0 or q > 0:
                        low_half(n - 1, 1 - q)
                        wait(dve, s_main, 3 * (n - 2) + 1)
                        products(prod_d[:, q, :], t, k, q, 1, DIRECT, i0, FIELDS - i0).then_inc(s_prod_d, 1)
                    if t > 0 and FIRST_SIDE < k0 <= LAST_SIDE and (k0 < LAST_SIDE or q == 0):
                        y_products(t - 1, k - FIRST_SIDE - 1, q)

            dve.wait_ge(s_zero, 4)
            run(dve, body)
            low_half(2 * BODIES * TILES - 1, 1)
            dve.wait_ge(s_mlpload, 80)
            nc.vector.tensor_tensor(w1_sb[:, 0, :], w1_sb[:, 0, :], w1_sb[:, 2, :], ALU.add).then_inc(s_w1, 1)
            softmax_max(TILES - 1)
            softmax_scale(TILES - 1)

            def tail_part(g):
                first, n = STACK * g, min(STACK * TGROUP, TILE - STACK * g)
                return first, n, 2 if n == STACK * TGROUP else 1, g // TGROUP

            def tail_products(g):
                first, n, halves, step = tail_part(g)
                bank = (ps_y, ps_sc)[step % 2]
                dve.wait_ge(s_tail_y, step + 1)
                wait(dve, s_tail_z, step - 1)
                rows_of = n // halves
                e = AP(tensor=emb[(TILES - 1) % 3], offset=first * WIDE,
                       ap=[[TILE * WIDE, 128], [rows_of * WIDE, halves], [WIDE, rows_of], [1, FIELDS]])
                nc.vector.tensor_tensor(
                    tail_tmp[:, step % 2, 0:n * FIELDS].rearrange("p (h b i) -> p h b i", h=halves, i=FIELDS), e,
                    bank[:, 0:halves, 0:rows_of * FIELDS].rearrange("p h (b i) -> p h b i", i=FIELDS),
                    ALU.mult).then_inc(s_tail_ymul, 1)

            def tail_sum(g):
                first, n, halves, step = tail_part(g)
                dve.wait_ge(s_tail_ymul, step + 1)
                nc.vector.tensor_reduce(zT[:, EARLY + first:EARLY + first + n],
                                        tail_tmp[:, step % 2, 0:n * FIELDS].rearrange("p (b i) -> p b i", i=FIELDS),
                                        axis=AX, op=ALU.add).then_inc(s_tail_z, 1)

            for g in range(0, TSTACKS, TGROUP):
                tail_products(g)
                if g > 0:
                    tail_sum(g - TGROUP)
            tail_sum(g)

        @block.scalar
        def _(act):
            def emb_copy(e, f, n, src):
                dst = AP(tensor=e, offset=f, ap=[[TILE * WIDE, 128], [1, n], [WIDE, TILE]])
                return nc.scalar.activation(dst, src, ACT.Copy)

            def emb_repeat(t, part, copied):
                act.wait_ge(s_copied, copied)
                v = emb[t % 3][:, :].rearrange("p (b f) -> p b f", f=WIDE)
                f, n = part * (SHIFTS // REPEATS), SHIFTS // REPEATS
                nc.scalar.activation(v[:, :, FIELDS + f:FIELDS + f + n], v[:, :, f:f + n], ACT.Copy).then_inc(s_emb, 1)

            def make_diag(t, copied):
                act.wait_ge(s_copied, copied)
                if t >= 2:
                    for q in range(2):
                        act.wait_ge(s_pick[q], 16 * BODIES * (t - 1))
                dst = AP(tensor=diag[t % 2], offset=0, ap=[[QUADS * 128, 128], [129, QUADS], [32, QUAD]])
                src = AP(tensor=gT, offset=TILE * t, ap=[[BATCH, 128], [1, QUADS], [32, QUAD]])
                nc.scalar.activation(dst, src, ACT.Copy).then_inc(s_diag, 1)

            act.wait_ge(s_xpose, 1)
            nc.scalar.activation(wT[:, :], ps[:, 0, 0:128], ACT.Copy).then_inc(s_split_w, 1)
            nc.scalar.activation(gT[:, 0:TILE], ps[:, 0, 128:256], ACT.Copy).then_inc(s_copied, 1)
            act.wait_ge(s_split_w, 1)
            nc.scalar.activation(w_hi[:, :], wT[:, :], ACT.Copy).then_inc(s_split_w, 1)
            act.wait_ge(s_zero, 4)
            make_diag(0, 1)
            for v in range(1, PRO):
                f, n = XFIELDS * (v - 1), min(XFIELDS, FIELDS - XFIELDS * (v - 1))
                act.wait_ge(s_xpose, v + 1)
                emb_copy(emb[0], f, n, ps[:, 2 * (v % 2), 0:n * TILE].rearrange("p (f b) -> p f b", b=TILE))\
                    .then_inc(s_copied, 1)
                if f + n == SHIFTS:
                    for part in range(REPEATS):
                        emb_repeat(0, part, v + 1)
            act.wait_ge(s_wload, 48)

            def relu(n, q, j, slot):
                act.wait_ge(s_main, 3 * n + j + 1)
                if j == 0:
                    wait(act, s_scores, n - 1)
                if j == 0:
                    dst = AP(tensor=fm, offset=q * QUAD * PAIRS,
                             ap=[[2 * QUAD * PAIRS, 128], [2 * PAIRS, 2], [PAIRS, 2], [1, DCOLS]])
                    src = ps[:, 2 * slot:2 * slot + 2, 0:2 * DCOLS].rearrange("p c (g n) -> p c g n", g=2)
                else:
                    dst = AP(tensor=fm, offset=q * QUAD * PAIRS + 2 * (j - 1) * PAIRS + DCOLS,
                             ap=[[2 * QUAD * PAIRS, 128], [PAIRS, 2], [1, SCOLS]])
                    src = ps[:, 2 * slot:2 * slot + 2, 0:SCOLS]
                nc.scalar.activation(dst, src, ACT.Relu, bias=attn_b_sb[:, 0:1]).then_inc(s_relu, 1)

            def high_half(n, q, h):
                act.wait_ge(s_prod_s, n + 1)
                wait(act, s_main, 3 * (n - 2) + 2 + h)
                wait(act, s_low, n - 1)
                part = slice(2 * SCOLS * h, 2 * SCOLS * (h + 1))
                nc.scalar.activation(high[:, q, part], prod_s[:, q, part], ACT.Copy).then_inc(s_high, 1)

            def scores_out(t):
                act.wait_ge(s_scores, QUADS * (t + 1))
                wait(act, s_exp, t)
                nc.scalar.activation(scores[:, :].rearrange("p (c n) -> p c n", c=2), ps_sc[:, :, 0:HALF],
                                     ACT.Copy).then_inc(s_sc_out, 1)

            def exponentials(t):
                act.wait_ge(s_max, t + 1)
                wait(act, s_square_out, 32 * t)
                nc.scalar.activation(expd[:, :], scores[:, :], ACT.Exp, bias=neg_max[:, 0:1],
                                     accum_out=total[:, 0:1]).then_inc(s_exp, 1)

            def drain_start(t, k, q):
                n = 2 * (BODIES * t + k) + q
                relu(n, q, 0, (3 * q) % 2)
                relu(n, q, 1, (3 * q + 1) % 2)

            def drain_end(t, k, k0, q):
                n = 2 * (BODIES * t + k) + q
                slot = q % 2
                relu(n, q, 2, slot)
                if side_x(t, k0):
                    v = PRO + SIDE * t + 2 * (k - FIRST_SIDE) + q
                    act.wait_ge(s_xpose, v + 1)
                    if k0 < LAST_SIDE:
                        emb_copy(emb[(t + 1) % 3], XFIELDS * (k - FIRST_SIDE) + 2 * q, 2,
                                 ps[:, 2 * slot:2 * slot + 2, SCOLS:SCOLS + TILE]).then_inc(s_copied, 1)
                    elif q == 0:
                        emb_copy(emb[(t + 1) % 3], FIELDS - 1, 1,
                                 ps[:, 2 * slot:2 * slot + 1, SCOLS:SCOLS + TILE]).then_inc(s_copied, 1)
                    else:
                        nc.scalar.activation(gT[:, TILE * (t + 1):TILE * (t + 2)],
                                             ps[:, 2 * slot, SCOLS:SCOLS + TILE], ACT.Copy).then_inc(s_copied, 1)
                        make_diag(t + 1, v + 1)
                if t < TILES - 1 and k0 in (LAST_SIDE - 1, LAST_SIDE):
                    emb_repeat(t + 1, 2 * (k0 - LAST_SIDE + 1) + q, PRO + SIDE * t + SHIFTS // 2)

            def body(t, k, k0, dt, dk, dk0):
                for q in range(2):
                    if dt >= 0:
                        drain_start(dt, dk, q)
                    if q == 0 and t > 0 and k0 == 1:
                        scores_out(t - 1)
                    high_half(2 * (BODIES * t + k) + q, q, 0)
                    if dt >= 0:
                        drain_end(dt, dk, dk0, q)
                    high_half(2 * (BODIES * t + k) + q, q, 1)
                    if q == 0 and t > 0 and k0 == 2:
                        exponentials(t - 1)

            for t, k, n in segments():
                if n == 1:
                    body(t, k, k, t if k else t - 1, (k - 1) % BODIES, (k - 1) % BODIES)
                else:
                    with act.Fori(0, n) as i:
                        body(t, k + i, k, t, k - 1 + i, k - 1)
            for q in range(2):
                drain_start(TILES - 1, BODIES - 1, q)
                drain_end(TILES - 1, BODIES - 1, BODIES - 1, q)
            scores_out(TILES - 1)
            act.wait_ge(s_mlpload, 80)
            exponentials(TILES - 1)

            def hidden1(c0, n, done, bank):
                for m in range(4):
                    act.wait_ge(s_mlp, done + m + 1)
                    nc.scalar.activation(h1[:, m * BATCH + c0:m * BATCH + c0 + n], bank(m), ACT.Relu,
                                         bias=b1_sb[:, m:m + 1]).then_inc(s_mlpact, 1)

            def hidden2(c0, n, done, bank):
                for m in range(2):
                    act.wait_ge(s_mlp, done + m + 1)
                    nc.scalar.activation(h2[:, m * BATCH + c0:m * BATCH + c0 + n], bank(m), ACT.Relu,
                                         bias=b2_sb[:, m:m + 1]).then_inc(s_mlpact, 1)

            hidden1(0, EARLY, 0, lambda m: ps[:, m, 0:EARLY])
            hidden2(0, EARLY, 4, lambda m: ps[:, m, 0:EARLY])
            act.wait_ge(s_mlp, 7)
            act.wait_ge(s_z, YSHARES * (TILES - 1))
            nc.scalar.activation(y_sb[:, 0:EARLY], ps[0:1, 2, 0:EARLY], ACT.Copy).then_inc(s_mlpact, 1)
            hidden1(EARLY, TILE, 7, lambda m: ps[:, m, 0:TILE])
            hidden2(EARLY, TILE, 11, lambda m: ps_y[:, m, 0:TILE])
            act.wait_ge(s_mlp, 14)
            nc.scalar.activation(y_sb[:, EARLY:BATCH], ps_sc[0:1, 0, 0:TILE], ACT.Copy).then_inc(s_mlpact, 1)

        @block.tensor
        def _(pe):
            pe.wait_ge(s_ident, 2)
            pe.wait_ge(s_wload, 48)
            nc.tensor.transpose(ps[:, 0, 0:128], wn[:, :], ident[:, :])
            nc.tensor.transpose(ps[:, 0, 128:256], gnn_sb[:, 0, :], ident[:, :]).then_inc(s_xpose, 1)
            for v in range(1, PRO):
                f, n = XFIELDS * (v - 1), min(XFIELDS, FIELDS - XFIELDS * (v - 1))
                pe.wait_ge(s_field[v - 1], 16 * n)
                if v >= 2:
                    pe.wait_ge(s_copied, v - 1)
                for c in range(n):
                    last = nc.tensor.transpose(ps[:, 2 * (v % 2), c * TILE:(c + 1) * TILE],
                                               rows[:, f + c, :], ident[:, :])
                last.then_inc(s_xpose, 1)
            pe.wait_ge(s_split_w, 3)

            def multiply(t, k, k0, q, steps):
                n = 2 * (BODIES * t + k) + q
                for j in steps:
                    m = 3 * n + j
                    slot = (3 * q + j) % 2
                    if j == 0:
                        pe.wait_ge(s_prod_d, n + 1)
                    if j == 1:
                        pe.wait_ge(s_low, n + 1)
                    if j < 2 and t == 0 and k0 == 0 and q == 0:
                        pe.wait_ge(s_copied, PRO)
                    elif j < 2 or not side_x(t, k0):
                        wait(pe, s_relu, m - 1)
                    if j == 1 and t < TILES - 1 and FIRST_SIDE <= k0 <= LAST_SIDE + 1 and (q == 0 or k0 <= LAST_SIDE):
                        pe.wait_ge(s_copied, PRO + SIDE * t + 2 * (k - FIRST_SIDE) + q)
                    if j == 0:
                        for c in range(2):
                            last = nc.tensor.matmul(ps[:, 2 * slot + c, 0:2 * DCOLS], wT[:, :],
                                                    prod_d[:, q, c * 2 * DCOLS:(c + 1) * 2 * DCOLS],
                                                    start=True, stop=True)
                    else:
                        for a, (w, p) in enumerate(((w_hi, high), (w_hi, low), (w_lo, high))):
                            for c in range(2):
                                g = 2 * (j - 1) + c
                                last = nc.tensor.matmul(ps[:, 2 * slot + c, 0:SCOLS], w[:, :],
                                                        p[:, q, g * SCOLS:(g + 1) * SCOLS],
                                                        start=(a == 0), stop=(a == 2))
                    last.then_inc(s_main, 1)

            def transposes(t, k, k0, q):
                slot = q % 2
                pe.wait_ge(s_relu, 3 * (2 * (BODIES * t + k) + q) + 1)
                if q == 0:
                    pe.wait_ge(s_stage, 16 * ((GROUPS + 1) * t + k - FIRST_SIDE + 1))
                if k0 < LAST_SIDE:
                    for c in range(2):
                        last = nc.tensor.transpose(ps[:, 2 * slot + c, SCOLS:SCOLS + TILE],
                                                   stage[:, (2 * q + c) * DIM:(2 * q + c + 1) * DIM], ident[:, :])
                elif q == 0:
                    last = nc.tensor.transpose(ps[:, 2 * slot, SCOLS:SCOLS + TILE], stage[:, 0:DIM], ident[:, :])
                else:
                    last = nc.tensor.transpose(ps[:, 2 * slot, SCOLS:SCOLS + TILE], gnn_sb[:, t + 1, :], ident[:, :])
                last.then_inc(s_xpose, 1)

            def score(n, q, first, last_quad):
                pe.wait_ge(s_relu, 3 * n + 3)
                for c in range(2):
                    for g in range(QUAD):
                        last = nc.tensor.matmul(ps_sc[32 * g:32 * g + 32, c, 0:HALF],
                                                pick[:, q, 32 * g:32 * g + 32],
                                                fm[:, q, g * PAIRS + c * HALF:g * PAIRS + (c + 1) * HALF],
                                                start=first, stop=last_quad)
                last.then_inc(s_scores, 1)

            def y_multiply(t, g, h):
                last_group = isinstance(g, int) and g == GROUPS - 1
                at = YSHARES * t + 2 * g + h
                loads = YLOADS[h] * (t + 1) if last_group else YLOADS[h] * t + (1 + STACK) * (g + 1)
                pe.wait_ge(s_yload[h], 16 * loads)
                wait(pe, s_ymul, at if isinstance(g, int) and g + h == 0 else at - 1)
                lanes = (YREST if last_group else STACK) * FIELDS
                for m in range(1 if last_group else YTRIPLES):
                    last = nc.tensor.matmul(ps_y[:, h, m * YCOLS:m * YCOLS + lanes], yrows[0:lanes, YTRIPLES * h + m, :],
                                            ymat[0:lanes, YTRIPLES * h + m, 0:lanes], start=True, stop=True)
                last.then_inc(s_y, 1)

            def body(t, k, k0):
                for q in range(2):
                    n = 2 * (BODIES * t + k) + q
                    multiply(t, k, k0, q, (0,))
                    if side_y(t, k0) and (k0 < LAST_SIDE - 1 or q == 0):
                        y_multiply(t - 1, k - FIRST_SIDE, q)
                    multiply(t, k, k0, q, (1,))
                    if t > 0 or k0 > 0 or q > 0:
                        pe.wait_ge(s_pick[1 - q], 16 * (BODIES * t + k + q))
                        first = k0 == 0 and q == 1
                        if first and t > 0:
                            pe.wait_ge(s_sc_out, t)
                        score(n - 1, 1 - q, first, k0 == 0 and q == 0)
                    if side_x(t, k0):
                        transposes(t, k, k0, q)
                    multiply(t, k, k0, q, (2,))

            run(pe, body)
            pe.wait_ge(s_pick[1], 16 * BODIES * TILES)
            score(2 * BODIES * TILES - 1, 1, False, True)

            def layer1(c0, n, m, chunks):
                for c in chunks:
                    last = nc.tensor.matmul(ps[:, m, 0:n], w1_sb[:, c, m * 128:(m + 1) * 128],
                                            (gT, zT)[c][:, c0:c0 + n], start=(c == 0), stop=(c == 1))
                if 1 in chunks:
                    last.then_inc(s_mlp, 1)

            def layer2(c0, n, bank, relus):
                for c in range(4):
                    pe.wait_ge(s_mlpact, relus + max(c + 1, 2))
                    for m in range(2):
                        last = nc.tensor.matmul(bank(m), w2_sb[:, c, m * 128:(m + 1) * 128],
                                                h1[:, c * BATCH + c0:c * BATCH + c0 + n], start=(c == 0), stop=(c == 3))
                        if c == 3:
                            last.then_inc(s_mlp, 1)

            def layer3(c0, n, bank, relus):
                for c in range(2):
                    pe.wait_ge(s_mlpact, relus + c + 1)
                    last = nc.tensor.matmul(bank, w3_sb[:, c:c + 1], h2[:, c * BATCH + c0:c * BATCH + c0 + n],
                                            start=(c == 0), stop=(c == 1))
                last.then_inc(s_mlp, 1)

            pe.wait_ge(s_mlpload, 80)
            pe.wait_ge(s_z, YSHARES * (TILES - 1))
            pe.wait_ge(s_relu, 3 * QUADS * TILES)
            pe.wait_ge(s_w1, 1)
            for m in range(4):
                layer1(0, EARLY, m, (0, 1))
            layer2(0, EARLY, lambda m: ps[:, m, 0:EARLY], 0)
            layer3(0, EARLY, ps[0:1, 2, 0:EARLY], 4)
            pe.wait_ge(s_tail_rows, 16 * STACK)
            pe.wait_ge(s_tail_mat, 16 * STACK)
            pe.wait_ge(s_sc_out, TILES)
            for g in range(0, TSTACKS, TGROUP):
                bank, step = (ps_y, ps_sc)[g // TGROUP % 2], g // TGROUP
                wait(pe, s_tail_ymul, step - 1)
                for at in range(g, min(g + TGROUP, TSTACKS)):
                    c, h = (at - g) % (TGROUP // 2), (at - g) // (TGROUP // 2)
                    lanes = min(STACK, TILE - STACK * at) * FIELDS
                    last = nc.tensor.matmul(bank[:, h, c * YCOLS:c * YCOLS + lanes],
                                            tail_rows[0:lanes, at, :], tail_mat[0:lanes, at, 0:lanes],
                                            start=True, stop=True)
                last.then_inc(s_tail_y, 1)
                if step in (1, 2):
                    pe.wait_ge(s_mlpact, 7)
                    for m in (2 * step - 2, 2 * step - 1):
                        layer1(EARLY, TILE, m, (0,))
            pe.wait_ge(s_tail_z, -(-TSTACKS // TGROUP))
            for m in range(4):
                layer1(EARLY, TILE, m, (1,))
            layer2(EARLY, TILE, lambda m: ps_y[:, m, 0:TILE], 7)
            layer3(EARLY, TILE, ps_sc[0:1, 0, 0:TILE], 11)


def kernel(**inputs):
    import numpy as _np
    import concourse.bacc as _bacc
    from concourse import mybir as _mybir
    from concourse.bass_utils import run_bass_kernel_spmd as _run

    nc = _bacc.Bacc("TRN2", target_bir_lowering=False, num_devices=1)
    arrays, aps = {}, {}
    for name, value in inputs.items():
        a = _np.ascontiguousarray(value)
        arrays[f"in_{name}_dram"] = a
        aps[name] = nc.dram_tensor(f"in_{name}_dram", a.shape, _mybir.dt.from_np(a.dtype), kind="ExternalInput").ap()
    out = nc.dram_tensor("out_0_dram", (BATCH, 1), _mybir.dt.float32, kind="ExternalOutput").ap()
    field_attention_tower(nc, aps["r_gnn_feature"], aps["ids"], [aps[f"tbl_{f}"] for f in range(FIELDS)],
                          aps["W_top1"], aps["b_top1"], aps["W_top2"], aps["b_top2"], aps["W_top3"],
                          aps["L0_rec_attn_W"], aps["L0_rec_attn_b"], out)
    r = _run(nc, [arrays], core_ids=[0])
    return r.results[0]["out_0_dram"]
```
